# Optimizing a Trainium2 kernel written in Bass

```python
import numpy as np
import jax
import jax.numpy as jnp

def _softmax(x, axis=-1):
    return jax.nn.softmax(x, axis=axis)

def _gelu(x):
    return jax.nn.gelu(x, approximate=True)

def _silu(x):
    return jax.nn.silu(x)

def _sigmoid(x):
    return jax.nn.sigmoid(x)

def _layernorm(x, axis=-1, eps=1e-05):
    m = jnp.mean(x, axis=axis, keepdims=True)
    v = jnp.var(x, axis=axis, keepdims=True)
    return (x - m) / jnp.sqrt(v + eps)

def _scatter_add(tgt, idx, src, axis=0):
    return tgt.at[idx].add(src)

def _segment_sum(src, seg, n):
    return jax.ops.segment_sum(src, seg, n)
kernel_name = 'mk_audio_tower_d1_tok_audfeat512_r4_ed8c6d'

def setup_inputs(seed: int=0):
    np.random.seed(seed)
    _w = jnp.asarray

    def _rec_inputs():
        import jax
        import jax.numpy as jnp
        _rk = jax.random.key(seed)
        x = -0.000392918 + 0.999932 * jax.random.normal(jax.random.fold_in(_rk, 1), (64, 375, 128), jnp.float32)
        return x
    x = _rec_inputs()

    def _L0_tok_setup():
        import jax, jax.numpy as jnp
        import numpy as np
        N_RECUR = 4
        STRIDE = 2
        key = jax.random.key(seed)
        ks = jax.random.split(key, 6)
        B, T, D = (16, 512, 128)
        glorot_mat = 1.0 / jnp.sqrt(D)
        return {'X': jax.random.normal(ks[0], (B, T, D), dtype=jnp.float32), 'W_in': jax.random.normal(ks[1], (N_RECUR, D, D), dtype=jnp.float32) * glorot_mat, 'b_in': jax.random.normal(ks[2], (N_RECUR, D), dtype=jnp.float32) * 0.05, 'W_out': jax.random.normal(ks[3], (N_RECUR, D, D), dtype=jnp.float32) * glorot_mat, 'b_out': jax.random.normal(ks[4], (N_RECUR, D), dtype=jnp.float32) * 0.05, 'core_diag': jax.random.normal(ks[5], (N_RECUR + 1, D), dtype=jnp.float32) * 0.05}
    _L0_tok_all = _L0_tok_setup()
    _L0_tok_in = {k: v for k, v in _L0_tok_all.items() if k in ('W_in', 'b_in', 'W_out', 'b_out', 'core_diag')}
    del _L0_tok_all

    def _L0_attn_setup():
        import jax, jax.numpy as jnp
        import numpy as np
        N_HEADS = 8
        D_MODEL = 128
        HEAD_DIM = D_MODEL // N_HEADS
        BATCH = 32
        SEQ = 128
        key = jax.random.key(seed)
        kx, kq, kv = jax.random.split(key, 3)
        x = jax.random.normal(kx, (BATCH, SEQ, D_MODEL), dtype=jnp.float32)
        Q = jax.random.uniform(kq, (N_HEADS, D_MODEL, D_MODEL), dtype=jnp.float32, minval=-0.1, maxval=0.1)
        V = jax.random.uniform(kv, (N_HEADS, D_MODEL, HEAD_DIM), dtype=jnp.float32, minval=-0.1, maxval=0.1)
        return {'input': x, 'Q': Q, 'V': V}
    _L0_attn_all = _L0_attn_setup()
    _L0_attn_in = {k: v for k, v in _L0_attn_all.items() if k in ('Q', 'V')}
    del _L0_attn_all

    def _L0_ffn_setup():
        import jax, jax.numpy as jnp
        import numpy as np
        E = 8
        K = 1
        D = 128
        I = 512
        B, T = (2, 512)
        key = jax.random.key(seed)
        ks = jax.random.split(key, 7)
        s = 0.02
        x = jax.random.normal(ks[0], (B, T, D), jnp.float32)
        gate_w = jax.random.normal(ks[1], (E, D), jnp.float32) * s
        w1 = jax.random.normal(ks[2], (E, I, D), jnp.float32) * s
        w2 = jax.random.normal(ks[3], (E, D, I), jnp.float32) * s
        w3 = jax.random.normal(ks[4], (E, I, D), jnp.float32) * s
        sw1 = jax.random.normal(ks[5], (I, D), jnp.float32) * s
        sw2 = jax.random.normal(ks[6], (D, I), jnp.float32) * s
        return {'x': x, 'gate_w': gate_w, 'w1': w1, 'w2': w2, 'w3': w3, 'sw1': sw1, 'sw2': sw2}
    _L0_ffn_all = _L0_ffn_setup()
    _L0_ffn_in = {k: v for k, v in _L0_ffn_all.items() if k in ('gate_w', 'w1', 'w2', 'w3', 'sw1', 'sw2')}
    del _L0_ffn_all
    return {'x': x, 'L0_tok_W_in': _L0_tok_in['W_in'], 'L0_tok_b_in': _L0_tok_in['b_in'], 'L0_tok_W_out': _L0_tok_in['W_out'], 'L0_tok_b_out': _L0_tok_in['b_out'], 'L0_tok_core_diag': _L0_tok_in['core_diag'], 'L0_attn_Q': _L0_attn_in['Q'], 'L0_attn_V': _L0_attn_in['V'], 'L0_ffn_gate_w': _L0_ffn_in['gate_w'], 'L0_ffn_w1': _L0_ffn_in['w1'], 'L0_ffn_w2': _L0_ffn_in['w2'], 'L0_ffn_w3': _L0_ffn_in['w3'], 'L0_ffn_sw1': _L0_ffn_in['sw1'], 'L0_ffn_sw2': _L0_ffn_in['sw2']}

def reference(x, L0_tok_W_in, L0_tok_b_in, L0_tok_W_out, L0_tok_b_out, L0_tok_core_diag, L0_attn_Q, L0_attn_V, L0_ffn_gate_w, L0_ffn_w1, L0_ffn_w2, L0_ffn_w3, L0_ffn_sw1, L0_ffn_sw2):
    import jax
    import jax.numpy as jnp

    def _L0_tok_ref(X, W_in, b_in, W_out, b_out, core_diag):
        import jax, jax.numpy as jnp
        import numpy as np
        N_RECUR = 4
        STRIDE = 2
        z_list = []
        z0 = jnp.tanh(jnp.abs(core_diag[0])[None, None, :] * X * X)
        z_list.append(z0)
        for i in range(N_RECUR):
            X = jnp.tanh(jnp.einsum('btd,de->bte', X, W_in[i]) + b_in[i])
            z = jnp.abs(core_diag[i + 1])[None, None, :] * X * X
            z_list.append(jnp.tanh(jnp.einsum('btd,de->bte', z, W_out[i]) + b_out[i]))
        out = jnp.mean(jnp.stack(z_list, axis=-2), axis=-2)
        B, T, D = out.shape
        Tp = T // STRIDE * STRIDE
        out_pool = out[:, :Tp].reshape(B, T // STRIDE, STRIDE, D).mean(axis=2)
        return out_pool

    def _L0_attn_ref(input, Q, V):
        import jax, jax.numpy as jnp
        import numpy as np
        N_HEADS = 8
        D_MODEL = 128
        HEAD_DIM = D_MODEL // N_HEADS
        BATCH = 32
        SEQ = 128
        scores = jnp.einsum('bnd,hde,bme->bhnm', input, Q, input)
        w = jax.nn.softmax(scores, axis=-1)
        weighted = jnp.einsum('bhnm,bmd->bhnd', w, input)
        out = jnp.einsum('bhnd,hdk->bhnk', weighted, V)
        B, H, N, K = out.shape
        return out.transpose(0, 2, 1, 3).reshape(B, N, H * K)

    def _L0_ffn_ref(x, gate_w, w1, w2, w3, sw1, sw2):
        import jax, jax.numpy as jnp
        import numpy as np
        E = 8
        K = 1
        D = 128
        I = 512
        B, T = (2, 512)
        xf = x.reshape(-1, D)
        logits = xf @ gate_w.T
        wts, idx = jax.lax.top_k(logits, K)
        wts = jax.nn.softmax(wts, axis=-1)
        comb = jnp.einsum('nke,nk->ne', jax.nn.one_hot(idx, E, dtype=xf.dtype), wts)
        h = jax.nn.silu(jnp.einsum('nd,eid->nei', xf, w1)) * jnp.einsum('nd,eid->nei', xf, w3)
        y = jnp.einsum('nei,edi->nd', h * comb[:, :, None], w2)
        y = y + jax.nn.gelu(xf @ sw1.T, approximate=False) @ sw2.T
        return y.reshape(x.shape)
    h = _L0_tok_ref(x, L0_tok_W_in, L0_tok_b_in, L0_tok_W_out, L0_tok_b_out, L0_tok_core_diag)
    h = h + _L0_attn_ref(_layernorm(h, axis=-1), L0_attn_Q, L0_attn_V)
    h = h + _L0_ffn_ref(_layernorm(h, axis=-1), L0_ffn_gate_w, L0_ffn_w1, L0_ffn_w2, L0_ffn_w3, L0_ffn_sw1, L0_ffn_sw2)
    return h

_drawn_inputs = setup_inputs


def setup_inputs(seed=0):
    import zlib

    import numpy as np

    out = dict(_drawn_inputs(seed))
    spreads = {}
    factors = {'L0_ffn_gate_w': 3.07, 'L0_ffn_w1': 3.304, 'L0_ffn_w2': 3.076, 'L0_ffn_w3': 3.259}
    for name, (base, spread) in spreads.items():
        noise = np.random.default_rng([zlib.crc32(name.encode()), seed]).standard_normal(out[name].shape)
        drawn = base * np.exp(spread * noise) if base else spread * noise
        out[name] = jnp.asarray(drawn.astype(out[name].dtype))
    for name, factor in factors.items():
        out[name] = (out[name] * factor).astype(out[name].dtype)
    return out
```

```python
from contextlib import ExitStack

import concourse.bass as bass
from concourse import mybir

F32 = mybir.dt.float32
BF16 = mybir.dt.bfloat16
I32 = mybir.dt.int32
U32 = mybir.dt.uint32
ALU = mybir.AluOpType
ACT = mybir.ActivationFunctionType
AX = mybir.AxisListType

D = 128
BATCH = 64
FRAMES = 374
TOK = FRAMES // 2
PAIRS = BATCH // 2
HALF = 192
COLS = 2 * HALF
RT = COLS // 128
M1 = TOK - 128
LAYERS = 4
HEADS = 8
HD = 16
VW = 32
E = 8
INNER = 512
NC = INNER // 128
TOKENS = BATCH * TOK
CAP_TILES = -(-TOKENS // 128)
CAP = CAP_TILES * 128
TILES = (TOKENS + E * 127) // 128
ROWS = PAIRS * COLS
NO_ROW = 1 << 20
EPS = 1e-5
FIRST_FULL, LAST_FULL = 2, PAIRS - 3


def wait(eng, sem, count):
    if not (isinstance(count, int) and count <= 0):
        eng.wait_ge(sem, count)


def wait_apart(eng, sem, count, met):
    if not isinstance(count, int):
        count = eng.to_reg(count)
        eng.wait_ge(met, 1)
    wait(eng, sem, count)


def iterations(eng, step):
    for it in range(-2, FIRST_FULL):
        step(it, it % 2)
    turns = (LAST_FULL - FIRST_FULL + 1) // 2
    with eng.Fori(0, turns) as turn:
        step(turn * 2 + FIRST_FULL, FIRST_FULL % 2)
        step(turn * 2 + (FIRST_FULL + 1), (FIRST_FULL + 1) % 2)
    for it in range(FIRST_FULL + 2 * turns, PAIRS + 1):
        step(it, it % 2)


def runs(pair):
    return not isinstance(pair, int) or 0 <= pair < PAIRS


def tower(nc, xT, w_in, b_in, w_out, b_out, core, q_w, v_w, gate_w, w1, w3, w2, sw1, sw2, out):
    ctx = ExitStack()
    with ctx:
        def sb(name, shape, dt=F32):
            return ctx.enter_context(nc.sbuf_tensor(name, shape, dt))

        def sem(name):
            return ctx.enter_context(nc.semaphore(name))

        w_in_sb = sb("w_in_sb", [128, LAYERS, D])
        w_out_sb = sb("w_out_sb", [128, LAYERS, D])
        w_out_c = sb("w_out_c", [128, LAYERS, D])
        b_in_sb = sb("b_in_sb", [128, LAYERS])
        b_out_sb = sb("b_out_sb", [128, LAYERS])
        core_sb = sb("core_sb", [128, LAYERS + 1])
        core_abs = sb("core_abs", [128, LAYERS + 1])
        q_sb = sb("q_sb", [128, HEADS, D])
        v_sb = sb("v_sb", [128, HEADS * HD])
        gate_sb = sb("gate_sb", [128, E])
        w1_sb = sb("w1_sb", [128, E * INNER])
        w3_sb = sb("w3_sb", [128, E * INNER])
        w2_sb = sb("w2_sb", [128, E * INNER])
        sw1_sb = sb("sw1_sb", [128, INNER])
        sw2_sb = sb("sw2_sb", [128, INNER])
        ident = sb("ident", [128, 128])
        before = sb("before", [128, 128], BF16)
        ones = sb("ones", [128, 128], BF16)
        minus_half = sb("minus_half", [128, RT])
        expert_no = sb("expert_no", [128, E])
        valid_hi = sb("valid_hi", [128, RT])
        valid = sb("valid", [128, RT])
        pad_far = sb("pad_far", [128, RT])
        xin = sb("xin", [128, 2, FRAMES])
        x_sq = sb("x_sq", [128, 2, FRAMES])
        xl = [sb(f"xl{i}", [128, 2, FRAMES]) for i in range(LAYERS)]
        sq = [sb(f"sq{i}", [128, 2, FRAMES]) for i in range(LAYERS)]
        z = [sb(f"z{i}", [128, 2, FRAMES]) for i in range(LAYERS + 1)]
        z_sum = sb("z_sum", [128, 2, FRAMES])
        pooled = sb("pooled", [128, COLS])
        h_raw = sb("h_raw", [128, RT, D])
        h_res = [sb(f"h_res{i}", [128, RT, D]) for i in range(2)]
        st1 = sb("st1", [128, RT, 6])
        mv1 = sb("mv1", [128, RT, 2])
        ve1 = sb("ve1", [128, RT])
        rstd1 = sb("rstd1", [128, RT])
        xn = sb("xn", [128, RT, D])
        xnT = [sb(f"xnT{i}", [128, COLS]) for i in range(2)]
        qx = [sb(f"qx{i}", [128, HEADS, COLS]) for i in range(2)]
        xv = [sb(f"xv{i}", [128, 4, HEADS, VW]) for i in range(2)]
        neg_max = sb("neg_max", [128, 2, RT])
        prob = [sb(f"prob{i}", [128, RT, TOK]) for i in range(2)]
        pT0 = sb("pT0", [128, HEADS, COLS])
        pT1 = sb("pT1", [M1, HEADS, COLS])
        oT = sb("oT", [128, 2, COLS])
        rden = sb("rden", [128, RT * 4])
        attn = sb("attn", [128, RT * 4, HD])
        rows = sb("rows", [128, RT, 2 * D])
        st2 = sb("st2", [128, RT, 6])
        mv2 = sb("mv2", [128, RT, 2])
        ve2 = sb("ve2", [128, RT])
        rstd2 = sb("rstd2", [128, RT])
        xn2T = sb("xn2T", [128, COLS])
        logits = sb("logits", [128, RT, E])
        top = sb("top", [128, RT, 8])
        top_i = sb("top_i", [128, RT, 8], U32)
        top_f = sb("top_f", [128, RT])
        is_top = sb("is_top", [128, RT, E])
        chosen = sb("chosen", [128, RT, E], BF16)
        place = sb("place", [128, RT, E])
        place_of = sb("place_of", [128, RT, E])
        place_f = sb("place_f", [128, RT])
        place_i = sb("place_i", [128, RT], I32)
        next_place = sb("next_place", [128, E])
        ids_f = sb("ids_f", [128, RT])
        ids = sb("ids", [128, RT], I32)
        no_rows = sb("no_rows", [128, (E + 1) * CAP // 128], I32)
        count_i = sb("count_i", [1, E], I32)
        ntile_i = sb("ntile_i", [1, E], I32)
        ntile = sb("ntile", [1, E])
        zero8 = sb("zero8", [1, E])
        list_start = sb("list_start", [1, E])
        count = sb("count", [1, E])
        ends = sb("ends", [1, E])
        tile_no = sb("tile_no", [1, TILES])
        past = sb("past", [1, TILES, E])
        past_n = sb("past_n", [1, TILES, E])
        t_exp = sb("t_exp", [1, TILES])
        t_skip = sb("t_skip", [1, TILES])
        t_row = sb("t_row", [1, TILES])
        t_row2 = sb("t_row2", [1, TILES])
        tab_row = sb("tab_row", [1, TILES], I32)
        tab_w = sb("tab_w", [1, TILES], I32)
        tile_ids = [sb(f"tile_ids{i}", [128, 1], I32) for i in range(4)]
        got = [z[i][:, :, :].rearrange("p a n -> p (a n)")[:, 0:2 * D] for i in range(4)]
        xgT = [xn[:, i, :] for i in range(2)]
        res = [h_raw[:, i, :] for i in range(2)]
        half_tanh, gate_u, hid, hidT, *shared = (
            m[:, :, :].rearrange("p a n -> p (a n)")[:, 0:INNER] for m in (*sq, xl[0], xl[1]))

        bank = [ctx.enter_context(nc.psum_tensor(f"bank{i}", [128, 512], F32)) for i in range(6)]
        score_ps = ctx.enter_context(nc.psum_tensor("score_ps", [128, 1024], F32))
        pT0_ps, pT1_ps, pv_ps, mix_ps, b_ps, d_ps = bank
        scores = score_ps[:, 0:RT * 256].rearrange("p (t n) -> p t n", t=RT)[:, :, 0:TOK]

        lists = nc.dram_tensor("lists", ((E + 1) * CAP, 1), I32, kind="Internal").ap()
        row_store = nc.dram_tensor("row_store", (ROWS, 2 * D), F32, kind="Internal").ap()

        s = {n: sem(n) for n in (
            "mixer_weights", "core_loaded", "attn_weights", "expert_weights", "shared_weights",
            "filled", "lists_cleared",
            "gp_const", "dve_const", "core_ready",
            "xin_loaded", "x_squared", "mix_mm", "mix_act", "z0_act", "squared", "z_added", "pooled_ok",
            "hT_tr", "h_out", "stat1", "mean1", "var1_eps", "rstd1_ok", "xn_ok", "xn_tr", "xnT_ok",
            "qx_mm", "qx_ok", "xv_mm", "xv_ok", "h_kept",
            "score_mm", "max_ok", "exp_ok", "pT_tr", "pT0_ok", "pT1_ok", "pv_mm", "oT_ok", "oT_tr",
            "rden_ok", "attn_ok", "h2_ok", "stat2", "mean2", "var2_eps", "rstd2_ok", "xn2_ok",
            "rows_stored", "xn2_tr", "xn2T_ok", "gate_mm", "logits_ok", "top_ok", "topi_ok", "topf_ok",
            "istop_ok", "chosen_ok", "rank_mm", "place_ok", "placeof_ok", "placef_ok", "placei_ok",
            "next_ok", "ids_stepped", "ids_ok", "scattered",
            "table_step", "table_ok",
            "up_mm", "sh_mm", "x_tr", "xgT_ok", "tanh_ok", "gelu_ok", "gate_ok", "hid_ok", "hid_tr",
            "hidT_ok", "down_mm", "res_ok")}
        ids_in = [sem(f"ids_in{i}") for i in range(4)]
        got_in = [sem(f"got_in{i}") for i in range(4)]
        stored = [sem(f"stored{i}") for i in range(2)]

        block = ctx.enter_context(nc.Block())

        @block.sync
        def _(sp):
            sp.dma_start(xin[:, :, :], xT[:, 0:2 * FRAMES].rearrange("p (a n) -> p a n", a=2)).then_inc(s["xin_loaded"], 16)
            sp.dma_start(w_in_sb[:, :, :], w_in).then_inc(s["mixer_weights"], 16)
            sp.dma_start(b_in_sb[:, :], b_in).then_inc(s["mixer_weights"], 16)
            sp.dma_start(b_out_sb[:, :], b_out).then_inc(s["mixer_weights"], 16)
            sp.dma_start(w_out_sb[:, :, :], w_out).then_inc(s["core_loaded"], 16)
            sp.dma_start(core_sb[:, :], core).then_inc(s["core_loaded"], 16)
            sp.dma_start(q_sb[:, :, :], q_w).then_inc(s["attn_weights"], 16)
            sp.dma_start(v_sb[:, :], v_w).then_inc(s["attn_weights"], 16)
            sp.dma_start(gate_sb[:, :], gate_w).then_inc(s["attn_weights"], 16)
            sp.dma_start(w1_sb[:, :], w1).then_inc(s["expert_weights"], 16)
            sp.dma_start(w3_sb[:, :], w3).then_inc(s["expert_weights"], 16)
            sp.dma_start(w2_sb[:, :], w2).then_inc(s["expert_weights"], 16)
            sp.dma_start(sw1_sb[:, :], sw1).then_inc(s["shared_weights"], 16)
            sp.dma_start(sw2_sb[:, :], sw2).then_inc(s["shared_weights"], 16)
            sp.wait_ge(s["filled"], 1)
            sp.dma_start(lists.rearrange("(p n) a -> p (n a)", p=128), no_rows[:, :]).then_inc(s["lists_cleared"], 16)

            def step(it, par):
                a, d = it + 2, it - 1
                nxt = a + 1
                if runs(nxt) and runs(a):
                    wait(sp, s["mix_mm"], a * 16 + 2)
                    wait(sp, s["x_squared"], a * 2 + 2)
                    src = xT[:, bass.ds(nxt * (2 * FRAMES), 2 * FRAMES)]
                    sp.dma_start(xin[:, :, :], src.rearrange("p (a n) -> p a n", a=2)).then_inc(s["xin_loaded"], 16)
                if runs(d):
                    wait(sp, s["xn2_ok"], d * RT + RT)
                    dst = row_store[bass.ds(d * COLS, COLS), :].rearrange("(t p) n -> p t n", p=128)
                    sp.dma_start(dst, rows[:, :, :]).then_inc(s["rows_stored"], 16)

            for it in range(-2, FIRST_FULL):
                step(it, it % 2)
            turns = (LAST_FULL - 1 - FIRST_FULL + 1)
            with sp.Fori(0, turns) as turn:
                step(turn + FIRST_FULL, 0)
            for it in range(FIRST_FULL + turns, PAIRS + 1):
                step(it, it % 2)

            sp.wait_ge(s["rows_stored"], 16 * PAIRS)
            sp.wait_ge(s["scattered"], 16 * PAIRS * RT)
            sp.wait_ge(s["table_ok"], 1)

            def load_ids(t, n):
                place_t = sp.value_load(tab_row[0:1, bass.ds(t, 1)], min_val=0, max_val=(E + 1) * CAP_TILES - 1)
                sp.dma_start(tile_ids[n][:, :], lists[bass.ds(place_t * 128, 128), :]).then_inc(ids_in[n], 16)

            for t in range(4):
                load_ids(t, t)
            with sp.Fori(1, TILES // 4) as r:
                for n in range(4):
                    sp.wait_ge(stored[n % 2], (r * 2 - 1 + n // 2) * 16)
                    load_ids(r * 4 + n, n)
            for t in range(TILES // 4 * 4, TILES):
                sp.wait_ge(stored[t % 2], ((t - 4) // 2 + 1) * 16)
                load_ids(t, t % 4)
            for par in range(2):
                sp.wait_ge(stored[par], 16 * ((TILES + 1 - par) // 2))

        @block.gpsimd
        def _(gp):
            gp.memset(no_rows[:, :], NO_ROW).then_inc(s["filled"], 1)
            gp.memset(ident[:, :], 0.0).then_inc(s["gp_const"], 1)
            gp.memset(before[:, :], 1.0).then_inc(s["gp_const"], 1)
            gp.memset(valid[:, :], 1.0).then_inc(s["gp_const"], 1)
            gp.memset(valid_hi[:, :], 0.0).then_inc(s["gp_const"], 1)
            gp.iota(ids_f[:, :], pattern=[[128, RT]], base=0, channel_multiplier=1,
                    allow_small_or_imprecise_dtypes=True)
            gp.iota(expert_no[:, :], pattern=[[1, E]], base=0, channel_multiplier=0,
                    allow_small_or_imprecise_dtypes=True)
            gp.iota(next_place[:, :], pattern=[[CAP, E]], base=0, channel_multiplier=0,
                    allow_small_or_imprecise_dtypes=True)
            gp.iota(list_start[:, :], pattern=[[CAP, E]], base=0, channel_multiplier=0,
                    allow_small_or_imprecise_dtypes=True)
            gp.iota(tile_no[:, :], pattern=[[1, TILES]], base=0, channel_multiplier=0,
                    allow_small_or_imprecise_dtypes=True).then_inc(s["gp_const"], 1)
            gp.wait_ge(s["gp_const"], 5)
            gp.affine_select(out=ident[:, :], in_=ident[:, :], compare_op=ALU.not_equal, fill=1.0,
                             base=0, pattern=[[-1, 128]], channel_multiplier=1).then_inc(s["gp_const"], 1)
            gp.affine_select(out=before[:, :], in_=before[:, :], compare_op=ALU.is_gt, fill=0.0,
                             base=0, pattern=[[1, 128]], channel_multiplier=-1).then_inc(s["gp_const"], 1)
            gp.affine_select(out=valid[:, 1:2], in_=valid[:, 1:2], compare_op=ALU.is_ge, fill=0.0,
                             base=M1 - 1, pattern=[[0, 1]], channel_multiplier=-1)
            gp.affine_select(out=valid[:, 2:3], in_=valid[:, 2:3], compare_op=ALU.is_ge, fill=0.0,
                             base=TOK - 64 - 1, pattern=[[0, 1]], channel_multiplier=-1)
            gp.affine_select(out=valid_hi[:, 1:2], in_=valid_hi[:, 1:2], compare_op=ALU.is_gt, fill=1.0,
                             base=64, pattern=[[0, 1]], channel_multiplier=-1).then_inc(s["gp_const"], 1)
            gp.wait_ge(s["dve_const"], 1)

            def step(it, par):
                a, b, d = it + 2, it + 1, it - 1
                for k in range(HEADS):
                    i = k // 2
                    if runs(a):
                        if k == 0:
                            wait(gp, s["xin_loaded"], a * 16 + 16)
                            wait(gp, s["z0_act"], a * 2)
                            for h in range(2):
                                gp.tensor_tensor(x_sq[:, h, :], xin[:, h, :], xin[:, h, :], ALU.mult)\
                                  .then_inc(s["x_squared"], 1)
                        for h in range(2):
                            if k % 2 == 0:
                                wait(gp, s["mix_act"], a * 16 + 4 * i + h + 1)
                                gp.tensor_tensor(sq[i][:, h, :], xl[i][:, h, :], xl[i][:, h, :], ALU.mult)\
                                  .then_inc(s["squared"], 1)
                            else:
                                wait(gp, s["mix_act"], a * 16 + 4 * i + h + 3)
                                if i == 0:
                                    wait(gp, s["z0_act"], a * 2 + h + 1)
                                    wait(gp, s["pooled_ok"], a * 2 + h - 1)
                                    left = z[0]
                                else:
                                    wait(gp, s["z_added"], a * 8 + 2 * (i - 1) + h + 1)
                                    left = z_sum
                                gp.tensor_tensor(z_sum[:, h, :], left[:, h, :], z[i + 1][:, h, :], ALU.add)\
                                  .then_inc(s["z_added"], 1)
                    if k == 0 and runs(b):
                        wait_apart(gp, s["mean1"], b * RT + RT, s["filled"])
                        gp.tensor_scalar(ve1[:, :], mv1[:, :, 1], EPS, None, ALU.add).then_inc(s["var1_eps"], 1)
                        wait(gp, s["var1_eps"], b + 1)
                        gp.tensor_tensor(rstd1[:, :], ve1[:, :], minus_half[:, :], ALU.pow).then_inc(s["rstd1_ok"], 1)
                    if k == 3 and runs(d):
                        wait_apart(gp, s["mean2"], d * RT + RT, s["filled"])
                        gp.tensor_scalar(ve2[:, :], mv2[:, :, 1], EPS, None, ALU.add).then_inc(s["var2_eps"], 1)
                        wait(gp, s["var2_eps"], d + 1)
                        gp.tensor_tensor(rstd2[:, :], ve2[:, :], minus_half[:, :], ALU.pow).then_inc(s["rstd2_ok"], 1)
                    if k == 4 and runs(b):
                        wait(gp, s["h_out"], b + 1)
                        wait_apart(gp, s["h2_ok"], (b - 1) * 2, s["filled"])
                        gp.tensor_copy(h_res[1 - par][:, :, :], h_raw[:, :, :]).then_inc(s["h_kept"], 1)
                    if k == 7 and runs(d):
                        wait_apart(gp, s["scattered"], d * RT * 16, s["filled"])
                        wait_apart(gp, s["ids_stepped"], d, s["filled"])
                        gp.tensor_copy(ids[:, :], ids_f[:, :]).then_inc(s["ids_ok"], 1)
                        wait_apart(gp, s["ids_ok"], d + 1, s["filled"])
                        gp.tensor_scalar(ids_f[:, :], ids_f[:, :], float(COLS), None, ALU.add).then_inc(s["ids_stepped"], 1)
                        wait_apart(gp, s["placei_ok"], d + 1, s["filled"])
                        if isinstance(d, int) and d == 0:
                            gp.wait_ge(s["lists_cleared"], 16)
                        for t in range(RT):
                            gp.indirect_dma_start(lists, bass.IndirectOffsetOnAxis(ap=place_i[:, t:t + 1], axis=0),
                                                  ids[:, t:t + 1], None, bounds_check=E * CAP - 1,
                                                  oob_is_err=False).then_inc(s["scattered"], 16)

            iterations(gp, step)

            gp.wait_ge(s["rows_stored"], 16 * PAIRS)

            def gather(t, n, turn):
                wait_apart(gp, ids_in[n], (turn + 1) * 16, s["filled"])
                wait_apart(gp, s["res_ok"], t - 3, s["filled"])
                gp.indirect_dma_start(got[n][:, :], None, row_store,
                                      bass.IndirectOffsetOnAxis(ap=tile_ids[n][:, :], axis=0),
                                      bounds_check=ROWS - 1, oob_is_err=False).then_inc(got_in[n], 16)

            def scatter(t, n):
                wait_apart(gp, s["res_ok"], t + 1, s["filled"])
                gp.indirect_dma_start(out, bass.IndirectOffsetOnAxis(ap=tile_ids[n][:, :], axis=0),
                                      res[n % 2][:, :], None, bounds_check=ROWS - 1,
                                      oob_is_err=False).then_inc(stored[n % 2], 16)

            gather(0, 0, 0)
            gather(1, 1, 0)
            gather(2, 2, 0)
            scatter(0, 0)
            gather(3, 3, 0)
            scatter(1, 1)
            with gp.Fori(1, TILES // 4) as r:
                for n in range(4):
                    gather(r * 4 + n, n, r)
                    scatter(r * 4 + (n - 2), (n - 2) % 4)
            for t in range(TILES // 4 * 4, TILES + 2):
                if t < TILES:
                    gather(t, t % 4, t // 4)
                scatter(t - 2, (t - 2) % 4)

        @block.scalar
        def _(act):
            act.wait_ge(s["mixer_weights"], 48)
            act.wait_ge(s["core_loaded"], 32)
            act.activation(core_abs[:, :], core_sb[:, :], ACT.Abs).then_inc(s["core_ready"], 1)
            act.wait_ge(s["core_ready"], 1)

            def mixer_tanh(a, u):
                i, outer, h = u // 4, (u // 2) % 2, u % 2
                wait(act, s["mix_mm"], a * 16 + u + 1)
                if u == 2:
                    wait(act, s["z_added"], a * 8)
                dst = z[i + 1] if outer else xl[i]
                bias = b_out_sb if outer else b_in_sb
                act.activation(dst[:, h, :], mix_ps[:, 0:FRAMES], ACT.Tanh, bias=bias[:, i:i + 1])\
                   .then_inc(s["mix_act"], 1)

            def step(it, par):
                a, c, d = it + 2, it, it - 1
                for k in range(HEADS):
                    if runs(a):
                        mixer_tanh(a, 2 * k)
                    if runs(c):
                        wait(act, s["max_ok"], c * 8 + k + 1)
                        wait(act, s["pT_tr"], (c * 8 + k - 1) * 2)
                        for t in range(RT):
                            e = act.activation(prob[k % 2][:, t, :], scores[:, t, :], ACT.Exp,
                                               bias=neg_max[:, k % 2, t:t + 1])
                        e.then_inc(s["exp_ok"], 1)
                    if runs(a):
                        mixer_tanh(a, 2 * k + 1)
                        if k == 0:
                            for h in range(2):
                                wait(act, s["x_squared"], a * 2 + h + 1)
                                if h == 0:
                                    wait(act, s["z_added"], a * 8)
                                act.activation(z[0][:, h, :], x_sq[:, h, :], ACT.Tanh, scale=core_abs[:, 0:1])\
                                   .then_inc(s["z0_act"], 1)
                    q, hd = (d, HEADS - 1) if k == 0 else (c, k - 1)
                    if runs(q):
                        wait(act, s["pT_tr"], (q * 8 + hd) * 2 + 2)
                        act.activation(pT1[:, hd, :], pT1_ps[0:M1, 0:COLS], ACT.Copy).then_inc(s["pT1_ok"], 1)

            iterations(act, step)

            def experts_act(t, par):
                wait(act, s["up_mm"], t * 2 + 1)
                wait(act, s["gate_ok"], t)
                act.activation(half_tanh[:, :], pT0_ps[:, :], ACT.Tanh, scale=0.5).then_inc(s["tanh_ok"], 1)
                wait(act, s["sh_mm"], t + 1)
                wait(act, s["down_mm"], t - 1)
                act.activation(shared[par][:, :], pv_ps[:, :], ACT.Gelu).then_inc(s["gelu_ok"], 1)

            def xgT_copy(t, par):
                wait(act, s["x_tr"], t + 1)
                act.activation(xgT[par][:, :], b_ps[:, 0:128], ACT.Copy).then_inc(s["xgT_ok"], 1)

            xgT_copy(0, 0)
            experts_act(0, 0)
            xgT_copy(1, 1)
            with act.Fori(0, (TILES - 2) // 2) as r:
                experts_act(r * 2 + 1, 1)
                xgT_copy(r * 2 + 2, 0)
                experts_act(r * 2 + 2, 0)
                xgT_copy(r * 2 + 3, 1)
            for t in range((TILES - 2) // 2 * 2 + 1, TILES):
                experts_act(t, t % 2)
                if t + 1 < TILES:
                    xgT_copy(t + 1, (t + 1) % 2)

        @block.vector
        def _(dve):
            dve.memset(ones[:, :], 1.0)
            dve.memset(minus_half[:, :], -0.5)
            dve.memset(zero8[:, :], 0.0)
            dve.memset(pooled[:, :], 0.0)
            for p in range(2):
                dve.memset(xv[p][:, :, :, 0:HD], 0.0)
                dve.memset(xv[p][:, :, :, HD:HD + 1], 1.0)
                dve.memset(xv[p][:, :, :, HD + 1:VW], 0.0)
            dve.memset(rden[:, :], 0.0).then_inc(s["dve_const"], 1)
            dve.wait_ge(s["core_ready"], 1)
            dve.wait_ge(s["core_loaded"], 32)
            for i in range(LAYERS):
                w = dve.tensor_scalar(w_out_c[:, i, :], w_out_sb[:, i, :], core_abs[:, i + 1:i + 2], None, ALU.mult)
            w.then_inc(s["core_ready"], 1)
            dve.wait_ge(s["gp_const"], 8)
            dve.tensor_tensor(valid[:, :], valid[:, :], valid_hi[:, :], ALU.add).then_inc(s["dve_const"], 1)
            dve.wait_ge(s["dve_const"], 2)
            dve.tensor_scalar(pad_far[:, :], valid[:, :], -float(NO_ROW), float(NO_ROW), ALU.mult, ALU.add)\
               .then_inc(s["dve_const"], 1)
            dve.wait_ge(s["dve_const"], 3)

            def layernorm(src, st, mv, stat, mean, n):
                for t in range(RT):
                    dve.bn_stats(st[:, t, :], src[t]).then_inc(s[stat], 1)
                for t in range(RT):
                    wait_apart(dve, s[stat], n * RT + t + 1, s["gp_const"])
                    dve.bn_aggr(mv[:, t, :], st[:, t, :]).then_inc(s[mean], 1)

            def merge(pair, g, p):
                tr = d_ps[:, 0:COLS].rearrange("p (n v) -> p n v", v=VW)
                wait(dve, s["oT_tr"], pair * 2 + g + 1)
                dve.reciprocal(rden[:, :], tr[:, :, HD]).then_inc(s["rden_ok"], 1)
                wait(dve, s["rden_ok"], pair * 2 + g + 1)
                dve.tensor_tensor(attn[:, :, :], tr[:, :, 0:HD],
                                  rden[:, :].rearrange("p (n o) -> p n o", o=1).to_broadcast([128, RT * 4, HD]),
                                  ALU.mult).then_inc(s["attn_ok"], 1)
                wait(dve, s["attn_ok"], pair * 2 + g + 1)
                wait(dve, s["h_kept"], pair + 1)
                if g == 0:
                    wait(dve, s["rows_stored"], pair * 16)
                dve.tensor_tensor(rows[:, :, D + 64 * g:D + 64 * g + 64],
                                  h_res[p][:, :, 64 * g:64 * g + 64],
                                  attn[:, :, :].rearrange("p (t h) v -> p t (h v)", t=RT),
                                  ALU.add).then_inc(s["h2_ok"], 1)

            def step(it, par):
                b, c, d = it + 1, it, it - 1
                for k in range(HEADS):
                    if runs(c):
                        wait(dve, s["score_mm"], c * 8 + k + 1)
                        dve.tensor_reduce(neg_max[:, k % 2, :], scores, AX.X, ALU.max, negate=True)\
                           .then_inc(s["max_ok"], 1)
                    q, hd = (d, HEADS - 1) if k == 0 else (c, k - 1)
                    if k == 0 and runs(b):
                        for h in range(2):
                            wait(dve, s["z_added"], b * 8 + 6 + h + 1)
                            if h == 0:
                                wait(dve, s["hT_tr"], b)
                            pairs = z_sum[:, h, :].rearrange("p (n two) -> p n two", two=2)
                            dve.tensor_tensor(pooled[:, h * HALF:h * HALF + TOK], pairs[:, :, 0], pairs[:, :, 1],
                                              ALU.add).then_inc(s["pooled_ok"], 1)
                    if runs(q):
                        wait(dve, s["pT_tr"], (q * 8 + hd) * 2 + 1)
                        dve.tensor_copy(pT0[:, hd, :], pT0_ps[:, 0:COLS]).then_inc(s["pT0_ok"], 1)
                    if k == 0 and runs(b):
                        wait(dve, s["hT_tr"], b + 1)
                        wait(dve, s["h_kept"], b)
                        dve.tensor_scalar(h_raw[:, :, :], b_ps[:, 0:COLS].rearrange("p (t n) -> p t n", t=RT),
                                          1.0 / (2 * (LAYERS + 1)), None, ALU.mult).then_inc(s["h_out"], 1)
                        wait(dve, s["h_out"], b + 1)
                        layernorm([h_raw[:, t, :] for t in range(RT)], st1, mv1, "stat1", "mean1", b)
                    if k == 1 and runs(b):
                        wait(dve, s["rstd1_ok"], b + 1)
                        for t in range(RT):
                            dve.tensor_scalar(xn[:, t, :], h_raw[:, t, :], mv1[:, t, 0:1], rstd1[:, t:t + 1],
                                              ALU.subtract, ALU.mult).then_inc(s["xn_ok"], 1)
                    if k == 2:
                        if runs(b):
                            wait(dve, s["xn_tr"], b + 1)
                            dve.tensor_copy(xnT[1 - par][:, :], b_ps[:, 0:COLS]).then_inc(s["xnT_ok"], 1)
                        if runs(d):
                            wait(dve, s["pv_mm"], d * 2 + 2)
                            dve.tensor_copy(oT[:, 1, :], pv_ps[:, 0:COLS]).then_inc(s["oT_ok"], 1)
                    if 3 <= k <= 6 and runs(b):
                        for j in (2 * (k - 3), 2 * (k - 3) + 1):
                            wait(dve, s["qx_mm"], b * 8 + j + 1)
                            dve.tensor_copy(qx[1 - par][:, j, :], b_ps[:, 0:COLS]).then_inc(s["qx_ok"], 1)
                    if k == 3 and runs(d):
                        merge(d, 1, 1 - par)
                        wait(dve, s["h2_ok"], d * 2 + 2)
                        layernorm([rows[:, t, D:2 * D] for t in range(RT)], st2, mv2, "stat2", "mean2", d)
                        wait(dve, s["rstd2_ok"], d + 1)
                        for t in range(RT):
                            dve.tensor_scalar(rows[:, t, 0:D], rows[:, t, D:2 * D], mv2[:, t, 0:1],
                                              rstd2[:, t:t + 1], ALU.subtract, ALU.mult).then_inc(s["xn2_ok"], 1)
                    if k == 5 and runs(d):
                        wait(dve, s["xn2_tr"], d + 1)
                        dve.tensor_copy(xn2T[:, :], d_ps[:, 0:COLS]).then_inc(s["xn2T_ok"], 1)
                    if k == 6:
                        if runs(c):
                            wait(dve, s["pv_mm"], c * 2 + 1)
                            dve.tensor_copy(oT[:, 0, :], pv_ps[:, 0:COLS]).then_inc(s["oT_ok"], 1)
                        if runs(d):
                            wait(dve, s["gate_mm"], d + 1)
                            dve.tensor_copy(logits[:, :, :], d_ps[:, 0:RT * E].rearrange("p (t e) -> p t e", t=RT))\
                               .then_inc(s["logits_ok"], 1)
                            wait_apart(dve, s["logits_ok"], d + 1, s["gp_const"])
                            for t in range(RT):
                                dve.max(top[:, t, :], logits[:, t, :]).then_inc(s["top_ok"], 1)
                            for t in range(RT):
                                wait_apart(dve, s["top_ok"], d * RT + t + 1, s["gp_const"])
                                dve.max_index(top_i[:, t, :], top[:, t, :], logits[:, t, :]).then_inc(s["topi_ok"], 1)
                            wait(dve, s["topi_ok"], d * RT + RT)
                            dve.tensor_copy(top_f[:, :], top_i[:, :, 0]).then_inc(s["topf_ok"], 1)
                            wait(dve, s["topf_ok"], d + 1)
                            dve.tensor_tensor(is_top[:, :, :],
                                              expert_no[:, :].rearrange("p (o e) -> p o e", o=1).to_broadcast([128, RT, E]),
                                              top_f[:, :].rearrange("p (t o) -> p t o", o=1).to_broadcast([128, RT, E]),
                                              ALU.is_equal).then_inc(s["istop_ok"], 1)
                            wait(dve, s["istop_ok"], d + 1)
                            dve.tensor_tensor(chosen[:, :, :], is_top[:, :, :],
                                              valid[:, :].rearrange("p (t o) -> p t o", o=1).to_broadcast([128, RT, E]),
                                              ALU.mult).then_inc(s["chosen_ok"], 1)
                    if k == 7:
                        if runs(b):
                            wait(dve, s["xv_mm"], b + 1)
                            src = b_ps[:, :].rearrange("p (c h v) -> p c h v", c=4, h=HEADS)
                            for c4, m in ((0, 128), (1, M1), (2, 128), (3, M1)):
                                v = dve.tensor_copy(xv[1 - par][0:m, c4, :, 0:HD], src[0:m, c4, :, :])
                            v.then_inc(s["xv_ok"], 1)
                        if runs(c):
                            merge(c, 0, par)
                        if runs(d):
                            wait(dve, s["rank_mm"], d + 1)
                            rank = d_ps[:, 0:RT * E].rearrange("p (t e) -> p t e", t=RT)
                            wait(dve, s["next_ok"], d)
                            dve.tensor_tensor(place[:, :, :], rank,
                                              next_place[:, :].rearrange("p (o e) -> p o e", o=1).to_broadcast([128, RT, E]),
                                              ALU.add).then_inc(s["place_ok"], 1)
                            wait(dve, s["place_ok"], d + 1)
                            dve.tensor_tensor(next_place[:, :], next_place[:, :], d_ps[:, RT * E:RT * E + E],
                                              ALU.add).then_inc(s["next_ok"], 1)
                            dve.tensor_tensor(place_of[:, :, :], place[:, :, :], chosen[:, :, :], ALU.mult)\
                               .then_inc(s["placeof_ok"], 1)
                            wait(dve, s["placeof_ok"], d + 1)
                            dve.tensor_reduce(place_f[:, :], place_of[:, :, :], AX.X, ALU.add).then_inc(s["placef_ok"], 1)
                            wait(dve, s["placef_ok"], d + 1)
                            wait(dve, s["scattered"], d * RT * 16)
                            dve.tensor_tensor(place_i[:, :], place_f[:, :], pad_far[:, :], ALU.add)\
                               .then_inc(s["placei_ok"], 1)

            iterations(dve, step)

            n = 0

            def done(ins):
                nonlocal n
                n += 1
                ins.then_inc(s["table_step"], 1)
                dve.wait_ge(s["table_step"], n)

            def over_tiles(ap):
                return ap.rearrange("p (o e) -> p o e", o=1).to_broadcast([1, TILES, E])

            dve.wait_ge(s["next_ok"], PAIRS)
            done(dve.tensor_tensor(count[:, :], next_place[0:1, :], list_start[:, :], ALU.subtract))
            done(dve.tensor_scalar(count_i[:, :], count[:, :], 127.0, None, ALU.add))
            done(dve.tensor_scalar(ntile_i[:, :], count_i[:, :], 7, None, ALU.arith_shift_right))
            done(dve.tensor_copy(ntile[:, :], ntile_i[:, :]))
            done(dve.tensor_tensor_scan(ends[:, :], ntile[:, :], zero8[:, :], 0.0, ALU.add, ALU.add))
            done(dve.tensor_tensor(past[:, :, :],
                                   tile_no[:, :].rearrange("p (t o) -> p t o", o=1).to_broadcast([1, TILES, E]),
                                   over_tiles(ends[:, :]), ALU.is_ge))
            done(dve.tensor_reduce(t_exp[:, :], past[:, :, :], AX.X, ALU.add))
            done(dve.tensor_tensor(past_n[:, :, :], past[:, :, :], over_tiles(ntile[:, :]), ALU.mult))
            done(dve.tensor_reduce(t_skip[:, :], past_n[:, :, :], AX.X, ALU.add))
            done(dve.tensor_tensor(t_row[:, :], tile_no[:, :], t_skip[:, :], ALU.subtract))
            done(dve.tensor_scalar(t_row2[:, :], t_exp[:, :], float(CAP_TILES), None, ALU.mult))
            done(dve.tensor_tensor(tab_row[:, :], t_row2[:, :], t_row[:, :], ALU.add))
            dve.tensor_scalar(tab_w[:, :], t_exp[:, :], float(E - 1), float(INNER), ALU.min, ALU.mult)\
               .then_inc(s["table_ok"], 1)

            def hidden(t, par):
                wait(dve, s["hid_ok"], t)
                wait(dve, s["tanh_ok"], t + 1)
                dve.scalar_tensor_tensor(gate_u[:, :], half_tanh[:, :], 1.0, pT0_ps[:, :], ALU.add, ALU.mult)\
                   .then_inc(s["gate_ok"], 1)
                wait(dve, s["gate_ok"], t + 1)
                wait(dve, s["up_mm"], t * 2 + 2)
                wait(dve, s["hid_tr"], t)
                dve.scalar_tensor_tensor(hid[:, :], gate_u[:, :], 0.5, pT1_ps[:, :], ALU.mult, ALU.mult)\
                   .then_inc(s["hid_ok"], 1)

            def finish(t, n):
                wait(dve, s["hid_tr"], t + 1)
                wait(dve, s["down_mm"], t)
                dve.tensor_copy(hidT[:, :], mix_ps[:, :]).then_inc(s["hidT_ok"], 1)
                wait(dve, s["down_mm"], t + 1)
                if n is None:
                    return
                dve.tensor_tensor(res[n % 2][:, :], got[n][:, D:2 * D], d_ps[:, 0:D], ALU.add).then_inc(s["res_ok"], 1)

            def result_free(t, par):
                if isinstance(t, int) and t < 2:
                    return
                dve.wait_ge(stored[par], (t // 2) * 16 if isinstance(t, int) else t)

            hidden(0, 0)
            for t in range(3):
                hidden(t + 1, (t + 1) % 2)
                result_free(t, t % 2)
                finish(t, t)
            with dve.Fori(0, (TILES - 4) // 4) as r:
                for m in range(4):
                    hidden(r * 4 + (m + 4), m % 2)
                    t4 = (m + 3) % 4
                    result_free((r * 2 + (m + 3) // 2) * 16, t4 % 2)
                    finish(r * 4 + (m + 3), t4)
            for t in range((TILES - 4) // 4 * 4 + 3, TILES):
                if t + 1 < TILES:
                    hidden(t + 1, (t + 1) % 2)
                result_free(t, t % 2)
                finish(t, t % 4)

        @block.tensor
        def _(pe):
            pe.wait_ge(s["mixer_weights"], 48)
            pe.wait_ge(s["core_ready"], 2)
            pe.wait_ge(s["gp_const"], 8)

            def mixer(a, u):
                i, outer, h = u // 4, (u // 2) % 2, u % 2
                wait(pe, s["mix_act"], a * 16 + u)
                if outer:
                    wait(pe, s["squared"], a * 8 + 2 * i + h + 1)
                    w, rhs = w_out_c, sq[i]
                else:
                    if i == 0:
                        wait(pe, s["xin_loaded"], a * 16 + 16)
                    w, rhs = w_in_sb, (xin if i == 0 else xl[i - 1])
                pe.matmul(mix_ps[:, 0:FRAMES], w[:, i, :], rhs[:, h, :], start=True, stop=True)\
                  .then_inc(s["mix_mm"], 1)

            def three_transposes(dst, src, done):
                for t in range(RT):
                    tr = pe.transpose(dst(t), src(t), ident[:, :])
                tr.then_inc(done, 1)

            def b_piece(b, k, p, late):
                if k == 0 and late:
                    wait(pe, s["pooled_ok"], b * 2 + 2)
                    wait(pe, s["xv_ok"], b)
                    three_transposes(lambda t: b_ps[:, t * 128:t * 128 + 128],
                                     lambda t: pooled[:, t * 128:t * 128 + 128], s["hT_tr"])
                if k == 2 and not late:
                    wait(pe, s["xn_ok"], b * RT + RT)
                    wait(pe, s["h_out"], b + 1)
                    three_transposes(lambda t: b_ps[:, t * 128:t * 128 + 128],
                                     lambda t: xn[:, t, :], s["xn_tr"])
                if 3 <= k <= 6:
                    j = 2 * (k - 3) + late
                    if j == 0:
                        wait(pe, s["xnT_ok"], b + 1)
                        if isinstance(b, int) and b == 0:
                            pe.wait_ge(s["attn_weights"], 48)
                    else:
                        wait(pe, s["qx_ok"], b * 8 + j)
                    pe.matmul(b_ps[:, 0:COLS], q_sb[:, j, :], xnT[p][:, :], start=True, stop=True)\
                      .then_inc(s["qx_mm"], 1)
                if k == 7 and not late:
                    wait(pe, s["qx_ok"], b * 8 + 8)
                    for c4, (m0, m) in enumerate(((0, 128), (128, M1), (HALF, 128), (HALF + 128, M1))):
                        v = pe.matmul(b_ps[0:m, c4 * 128:c4 * 128 + 128], xnT[p][:, m0:m0 + m], v_sb[:, :],
                                      start=True, stop=True)
                    v.then_inc(s["xv_mm"], 1)

            def scores_of(c, h, p):
                if h == 0:
                    wait(pe, s["xv_ok"], c + 1)
                wait(pe, s["exp_ok"], c * 8 + h)
                qh, keys = qx[p][:, h, :], (xnT[p][:, 0:TOK], xnT[p][:, HALF:HALF + TOK])
                pe.matmul(scores[:, 0, :], qh[:, 0:128], keys[0], start=True, stop=True)
                pe.matmul(scores[:, 2, :], qh[:, 256:384], keys[1], start=True, stop=True)
                pe.matmul(scores[0:64, 1, :], qh[:, 128:192], keys[0], start=True, stop=True)
                pe.matmul(scores[64:128, 1, :], qh[:, 192:256], keys[1], start=True, stop=True)\
                  .then_inc(s["score_mm"], 1)

            def probs_T(q, h):
                wait(pe, s["exp_ok"], q * 8 + h + 1)
                wait(pe, s["pT0_ok"], q * 8 + h)
                three_transposes(lambda t: pT0_ps[:, t * 128:t * 128 + 128],
                                 lambda t: prob[h % 2][:, t, 0:128], s["pT_tr"])
                wait_apart(pe, s["pT1_ok"], q * 8 + h, s["gp_const"])
                three_transposes(lambda t: pT1_ps[0:M1, t * 128:t * 128 + 128],
                                 lambda t: prob[h % 2][:, t, 128:TOK], s["pT_tr"])

            def weighted(q, g, p):
                wait(pe, s["pT0_ok"], q * 8 + 4 * g + 4)
                wait(pe, s["pT1_ok"], q * 8 + 4 * g + 4)
                wait(pe, s["oT_ok"], q * 2 + g)
                for half in range(2):
                    cols = slice(half * HALF, half * HALF + HALF)
                    for chunk, (m, src) in enumerate(((128, pT0), (M1, pT1))):
                        for j in range(4):
                            h = 4 * g + j
                            v = pe.matmul(pv_ps[32 * j:32 * j + VW, cols], xv[p][0:m, 2 * half + chunk, h, :],
                                          src[0:m, h, cols], start=(chunk == 0), stop=(chunk == 1))
                v.then_inc(s["pv_mm"], 1)

            def heads_T(q, g):
                wait(pe, s["oT_ok"], q * 2 + g + 1)
                three_transposes(lambda t: d_ps[:, t * 128:t * 128 + 128],
                                 lambda t: oT[:, g, t * 128:t * 128 + 128], s["oT_tr"])

            def step(it, par):
                a, b, c, d = it + 2, it + 1, it, it - 1
                for k in range(HEADS):
                    if runs(c):
                        scores_of(c, k, par)
                    if runs(a):
                        mixer(a, 2 * k)
                    if runs(b):
                        b_piece(b, k, 1 - par, 0)
                    q, h = (d, HEADS - 1) if k == 0 else (c, k - 1)
                    if runs(q):
                        probs_T(q, h)
                    if runs(a):
                        mixer(a, 2 * k + 1)
                    if runs(b):
                        b_piece(b, k, 1 - par, 1)
                    if runs(d):
                        if k == 1:
                            weighted(d, 1, 1 - par)
                        if k == 2:
                            wait(pe, s["placei_ok"], d)
                            wait(pe, s["attn_ok"], d * 2 + 1)
                            heads_T(d, 1)
                        if k == 4:
                            wait(pe, s["xn2_ok"], d * RT + RT)
                            three_transposes(lambda t: d_ps[:, t * 128:t * 128 + 128],
                                             lambda t: rows[:, t, 0:D], s["xn2_tr"])
                        if k == 5:
                            wait(pe, s["xn2T_ok"], d + 1)
                            for t in range(RT):
                                g = pe.matmul(d_ps[:, t * E:t * E + E], xn2T[:, t * 128:t * 128 + 128],
                                              gate_sb[:, :], start=True, stop=True)
                            g.then_inc(s["gate_mm"], 1)
                    if runs(c) and k == 5:
                        weighted(c, 0, par)
                    if k == 6 and runs(c):
                        if runs(d):
                            wait(pe, s["logits_ok"], d + 1)
                        heads_T(c, 0)
                    if k == 7 and runs(d):
                        wait(pe, s["chosen_ok"], d + 1)
                        if runs(c):
                            wait(pe, s["attn_ok"], c * 2 + 1)
                        for t in range(RT):
                            for t2 in range(t):
                                pe.matmul(d_ps[:, t * E:t * E + E], ones[:, :], chosen[:, t2, :],
                                          start=(t2 == 0), stop=False)
                            pe.matmul(d_ps[:, t * E:t * E + E], before[:, :], chosen[:, t, :],
                                      start=(t == 0), stop=True)
                        for t in range(RT):
                            m = pe.matmul(d_ps[:, RT * E:RT * E + E], ones[:, :], chosen[:, t, :],
                                          start=(t == 0), stop=(t == RT - 1))
                        m.then_inc(s["rank_mm"], 1)

            iterations(pe, step)

            pe.wait_ge(s["expert_weights"], 48)
            pe.wait_ge(s["shared_weights"], 32)
            pe.wait_ge(s["table_ok"], 1)

            def expert(t):
                return pe.value_load(tab_w[0:1, bass.ds(t, 1)], min_val=0, max_val=(E - 1) * INNER)

            def rows_T(t, n, turn):
                pe.wait_ge(got_in[n], (turn + 1) * 16)
                wait(pe, s["xgT_ok"], t)
                pe.transpose(b_ps[:, 0:128], got[n][:, 0:D], ident[:, :]).then_inc(s["x_tr"], 1)

            def up(t, par, w):
                wait(pe, s["xgT_ok"], t + 1)
                wait(pe, s["gate_ok"], t)
                pe.matmul(pT0_ps[:, :], xgT[par][:, :], w1_sb[:, bass.ds(w, INNER)], start=True, stop=True)\
                  .then_inc(s["up_mm"], 1)
                wait(pe, s["hid_ok"], t)
                pe.matmul(pT1_ps[:, :], xgT[par][:, :], w3_sb[:, bass.ds(w, INNER)], start=True, stop=True)\
                  .then_inc(s["up_mm"], 1)
                wait(pe, s["gelu_ok"], t)
                for c in range(NC):
                    m = pe.matmul(pv_ps[:, c * 128:c * 128 + 128], sw1_sb[:, c * 128:c * 128 + 128],
                                  xgT[par][:, :], start=True, stop=True)
                m.then_inc(s["sh_mm"], 1)

            def down(t, par, w):
                wait(pe, s["gelu_ok"], t + 1)
                wait(pe, s["res_ok"], t)
                for c in range(NC):
                    pe.matmul(d_ps[:, 0:D], shared[par][:, c * 128:c * 128 + 128],
                              sw2_sb[:, c * 128:c * 128 + 128], start=(c == 0), stop=False)
                wait(pe, s["hid_ok"], t + 1)
                wait(pe, s["hidT_ok"], t)
                for c in range(NC):
                    tr = pe.transpose(mix_ps[:, c * 128:c * 128 + 128], hid[:, c * 128:c * 128 + 128], ident[:, :])
                tr.then_inc(s["hid_tr"], 1)
                wait(pe, s["hidT_ok"], t + 1)
                for c in range(NC):
                    m = pe.matmul(d_ps[:, 0:D], hidT[:, c * 128:c * 128 + 128],
                                  w2_sb[:, bass.ds(w + c * 128, 128)], start=False, stop=(c == NC - 1))
                m.then_inc(s["down_mm"], 1)

            rows_T(0, 0, 0)
            up(0, 0, expert(0))
            for t in range(3):
                rows_T(t + 1, t + 1, 0)
                up(t + 1, (t + 1) % 2, expert(t + 1))
                down(t, t % 2, expert(t))
            with pe.Fori(0, (TILES - 4) // 4) as r:
                for m in range(4):
                    rows_T(r * 4 + (m + 4), m, r + 1)
                    up(r * 4 + (m + 4), m % 2, expert(r * 4 + (m + 4)))
                    down(r * 4 + (m + 3), (m + 3) % 2, expert(r * 4 + (m + 3)))
            for t in range((TILES - 4) // 4 * 4 + 3, TILES):
                if t + 1 < TILES:
                    rows_T(t + 1, (t + 1) % 4, (t + 1) // 4)
                    up(t + 1, (t + 1) % 2, expert(t + 1))
                down(t, t % 2, expert(t))


def kernel(**inputs):
    import numpy as np
    import concourse.bacc as bacc
    from concourse.bass_utils import run_bass_kernel_spmd

    def lay(name, *order):
        return np.asarray(inputs[name]).transpose(order)

    x = np.asarray(inputs["x"])[:, :FRAMES, :]
    arrays = {
        "xT": x.transpose(2, 0, 1).reshape(D, BATCH * FRAMES),
        "w_in": lay("L0_tok_W_in", 1, 0, 2),
        "b_in": lay("L0_tok_b_in", 1, 0),
        "w_out": lay("L0_tok_W_out", 1, 0, 2),
        "b_out": lay("L0_tok_b_out", 1, 0),
        "core": lay("L0_tok_core_diag", 1, 0),
        "q_w": lay("L0_attn_Q", 1, 0, 2),
        "v_w": lay("L0_attn_V", 1, 0, 2).reshape(D, HEADS * HD),
        "gate_w": lay("L0_ffn_gate_w", 1, 0),
        "w1": lay("L0_ffn_w1", 2, 0, 1).reshape(D, E * INNER),
        "w3": lay("L0_ffn_w3", 2, 0, 1).reshape(D, E * INNER),
        "w2": np.asarray(inputs["L0_ffn_w2"]).reshape(E, D, NC, 128).transpose(3, 0, 2, 1).reshape(128, E * INNER),
        "sw1": lay("L0_ffn_sw1", 1, 0),
        "sw2": np.asarray(inputs["L0_ffn_sw2"]).reshape(D, NC, 128).transpose(2, 1, 0).reshape(128, INNER),
    }
    nc = bacc.Bacc("TRN2", target_bir_lowering=False, num_devices=1)
    feed, args = {}, []
    for name, a in arrays.items():
        a = np.ascontiguousarray(a)
        feed[f"in_{name}"] = a
        args.append(nc.dram_tensor(f"in_{name}", a.shape, mybir.dt.from_np(a.dtype), kind="ExternalInput").ap())
    args.append(nc.dram_tensor("out_rows", (ROWS, D), F32, kind="ExternalOutput").ap())
    tower(nc, *args)
    r = run_bass_kernel_spmd(nc, [feed], core_ids=[0])
    rows = r.results[0]["out_rows"].reshape(BATCH, HALF, D)
    return rows[:, :TOK, :]
```

```python
from contextlib import ExitStack

import concourse.bass as bass
from concourse import mybir

F32 = mybir.dt.float32
BF16 = mybir.dt.bfloat16
I32 = mybir.dt.int32
U32 = mybir.dt.uint32
ALU = mybir.AluOpType
ACT = mybir.ActivationFunctionType
AX = mybir.AxisListType

D = 128
BATCH = 64
FRAMES = 374
TOK = FRAMES // 2
PAIRS = BATCH // 2
HALF = 192
COLS = 2 * HALF
RT = COLS // 128
M1 = TOK - 128
LAYERS = 4
HEADS = 8
HD = 16
VW = 32
E = 8
INNER = 512
NC = INNER // 128
TOKENS = BATCH * TOK
CAP_TILES = -(-TOKENS // 128)
CAP = CAP_TILES * 128
TILES = (TOKENS + E * 127) // 128
ROWS = PAIRS * COLS
NO_ROW = 1 << 20
EPS = 1e-5
FIRST_FULL, LAST_FULL = 4, PAIRS - 4
BANKED = 4
LISTED = 8


def wait(eng, sem, count):
    if not (isinstance(count, int) and count <= 0):
        eng.wait_ge(sem, count)


def wait_apart(eng, sem, count, met):
    if not isinstance(count, int):
        count = eng.to_reg(count)
        eng.wait_ge(met, 1)
    wait(eng, sem, count)


def iterations(eng, step):
    for it in range(-2, FIRST_FULL):
        step(it, it % 2)
    turns = (LAST_FULL - FIRST_FULL + 1) // 2
    with eng.Fori(0, turns) as turn:
        step(turn * 2 + FIRST_FULL, FIRST_FULL % 2)
        step(turn * 2 + (FIRST_FULL + 1), (FIRST_FULL + 1) % 2)
    for it in range(FIRST_FULL + 2 * turns, PAIRS + 2):
        step(it, it % 2)


def tiles(eng, step):
    for t in range(LISTED):
        step(t, t, 0)
    with eng.Fori(1, TILES // LISTED - 1) as turn:
        for n in range(LISTED):
            step(turn * LISTED + n, n, turn)
    for t in range((TILES // LISTED - 1) * LISTED, TILES):
        step(t, t % LISTED, t // LISTED)


def has(tile):
    return not isinstance(tile, int) or 0 <= tile < TILES


def runs(pair):
    return not isinstance(pair, int) or 0 <= pair < PAIRS


def tower(nc, xT, w_in, b_in, w_out, b_out, core, q_w, v_w, gate_w, w1, w3, w2, sw1, sw2, out):
    ctx = ExitStack()
    with ctx:
        def sb(name, shape, dt=F32):
            return ctx.enter_context(nc.sbuf_tensor(name, shape, dt))

        def sem(name):
            return ctx.enter_context(nc.semaphore(name))

        w_in_sb = sb("w_in_sb", [128, LAYERS, D])
        w_out_sb = sb("w_out_sb", [128, LAYERS, D])
        w_out_c = sb("w_out_c", [128, LAYERS, D])
        b_in_sb = sb("b_in_sb", [128, LAYERS])
        b_out_sb = sb("b_out_sb", [128, LAYERS])
        core_sb = sb("core_sb", [128, LAYERS + 1])
        core_abs = sb("core_abs", [128, LAYERS + 1])
        q_sb = sb("q_sb", [128, HEADS, D])
        v_sb = sb("v_sb", [128, HEADS * HD])
        gate_sb = sb("gate_sb", [128, E])
        w1_sb = sb("w1_sb", [128, E * INNER])
        w3_sb = sb("w3_sb", [128, E * INNER])
        w2_sb = sb("w2_sb", [128, E * INNER])
        sw1_sb = sb("sw1_sb", [128, INNER])
        sw2_sb = sb("sw2_sb", [128, INNER])
        ident = sb("ident", [128, 128])
        before = sb("before", [128, 128], BF16)
        ones = sb("ones", [128, 128], BF16)
        minus_half = sb("minus_half", [128, RT])
        expert_no = sb("expert_no", [128, E])
        valid_hi = sb("valid_hi", [128, RT])
        valid = sb("valid", [128, RT])
        pad_far = sb("pad_far", [128, RT])
        xin = sb("xin", [128, 2, FRAMES])
        x_sq = sb("x_sq", [128, 2, FRAMES])
        xl = [sb(f"xl{i}", [128, 2, FRAMES]) for i in range(LAYERS)]
        sq = [sb(f"sq{i}", [128, 2, FRAMES]) for i in range(LAYERS)]
        z = [sb(f"z{i}", [128, 2, FRAMES]) for i in range(LAYERS + 1)]
        z_sum = sb("z_sum", [128, 2, FRAMES])
        pooled = sb("pooled", [128, COLS])
        h_raw = sb("h_raw", [128, RT, D])
        h_res = [sb(f"h_res{i}", [128, RT, D]) for i in range(2)]
        st1 = sb("st1", [128, RT, 6])
        mv1 = sb("mv1", [128, RT, 2])
        ve1 = sb("ve1", [128, RT])
        rstd1 = sb("rstd1", [128, RT])
        xn = sb("xn", [128, RT, D])
        xnT = [sb(f"xnT{i}", [128, COLS]) for i in range(2)]
        qx = [sb(f"qx{i}", [128, HEADS, COLS]) for i in range(2)]
        xv = [sb(f"xv{i}", [128, 4, HEADS, VW]) for i in range(2)]
        neg_max = sb("neg_max", [128, 2, RT])
        prob = [sb(f"prob{i}", [128, RT, TOK]) for i in range(2)]
        pT0 = sb("pT0", [128, HEADS, COLS])
        pT1 = sb("pT1", [M1, HEADS, COLS])
        oT = sb("oT", [128, 2, COLS])
        rden = sb("rden", [128, RT * 4])
        attn = sb("attn", [128, RT * 4, HD])
        rows = sb("rows", [128, RT, 2 * D])
        st2 = sb("st2", [128, RT, 6])
        mv2 = sb("mv2", [128, RT, 2])
        ve2 = sb("ve2", [128, RT])
        rstd2 = sb("rstd2", [128, RT])
        xn2T = sb("xn2T", [128, COLS])
        logits = sb("logits", [128, RT, E])
        top = sb("top", [128, RT, 8])
        top_i = sb("top_i", [128, RT, 8], U32)
        top_f = sb("top_f", [128, RT])
        is_top = sb("is_top", [128, RT, E])
        chosen = sb("chosen", [128, RT, E], BF16)
        place = sb("place", [128, RT, E])
        place_of = sb("place_of", [128, RT, E])
        place_f = sb("place_f", [128, RT])
        place_i = sb("place_i", [128, RT], I32)
        next_place = sb("next_place", [128, E])
        ids_f = sb("ids_f", [128, RT])
        ids = sb("ids", [128, RT], I32)
        no_rows = sb("no_rows", [128, (E + 1) * CAP // 128], I32)
        count_i = sb("count_i", [1, E], I32)
        ntile_i = sb("ntile_i", [1, E], I32)
        ntile = sb("ntile", [1, E])
        zero8 = sb("zero8", [1, E])
        list_start = sb("list_start", [1, E])
        count = sb("count", [1, E])
        ends = sb("ends", [1, E])
        tile_no = sb("tile_no", [1, TILES])
        past = sb("past", [1, TILES, E])
        past_n = sb("past_n", [1, TILES, E])
        t_exp = sb("t_exp", [1, TILES])
        t_skip = sb("t_skip", [1, TILES])
        t_row = sb("t_row", [1, TILES])
        t_row2 = sb("t_row2", [1, TILES])
        tab_row = sb("tab_row", [1, TILES], I32)
        tab_w = sb("tab_w", [1, TILES], I32)
        tile_ids = [sb(f"tile_ids{i}", [128, 1], I32) for i in range(LISTED)]
        got = [z[i][:, :, :].rearrange("p a n -> p (a n)")[:, 0:2 * D] for i in range(BANKED)]
        xgT = [xn[:, i, :] for i in range(2)]
        res = [h_raw[:, i, :] for i in range(2)]
        half_tanh, gate_u, hidT, *double = (
            m[:, :, :].rearrange("p a n -> p (a n)")[:, 0:INNER] for m in (*sq, *xl[0:3]))
        hid, shared = double[0:2], double[2:4]

        bank = [ctx.enter_context(nc.psum_tensor(f"bank{i}", [128, 512], F32)) for i in range(6)]
        score_ps = ctx.enter_context(nc.psum_tensor("score_ps", [128, 1024], F32))
        pT0_ps, pT1_ps, pv_ps, mix_ps, b_ps, d_ps = bank
        up_ps = (pT0_ps, pT1_ps, score_ps[:, 0:512], score_ps[:, 512:1024])
        sh_ps, hidT_ps, y_ps = pv_ps, mix_ps, d_ps
        scores = score_ps[:, 0:RT * 256].rearrange("p (t n) -> p t n", t=RT)[:, :, 0:TOK]

        lists = nc.dram_tensor("lists", ((E + 1) * CAP, 1), I32, kind="Internal").ap()
        row_store = nc.dram_tensor("row_store", (ROWS, 2 * D), F32, kind="Internal").ap()

        s = {n: sem(n) for n in (
            "mixer_weights", "core_loaded", "attn_weights", "expert_weights", "shared_weights",
            "filled", "lists_cleared",
            "gp_const", "dve_const", "core_ready",
            "xin_loaded", "x_squared", "mix_mm", "mix_act", "z0_act", "squared", "z_added", "pooled_ok",
            "hT_tr", "h_out", "stat1", "mean1", "var1_eps", "rstd1_ok", "xn_ok", "xn_tr", "xnT_ok",
            "qx_mm", "qx_ok", "xv_mm", "xv_ok", "h_kept",
            "score_mm", "max_ok", "exp_ok", "pT_tr", "pT0_ok", "pT1_ok", "pv_mm", "oT_ok", "oT_tr",
            "rden_ok", "attn_ok", "h2_ok", "stat2", "mean2", "var2_eps", "rstd2_ok", "xn2_ok",
            "rows_stored", "xn2_tr", "xn2T_ok", "gate_mm", "logits_ok", "top_ok", "topi_ok", "topf_ok",
            "istop_ok", "chosen_ok", "rank_mm", "place_ok", "placeof_ok", "placef_ok", "placei_ok",
            "next_ok", "ids_stepped", "ids_ok", "scattered",
            "table_step", "table_ok",
            "up_mm", "sh_mm", "x_tr", "xgT_ok", "tanh_ok", "gelu_ok", "gate_ok", "hid_ok", "hid_tr",
            "hidT_ok", "down_mm", "res_ok")}
        ids_in = [sem(f"ids_in{i}") for i in range(LISTED)]
        got_in = [sem(f"got_in{i}") for i in range(BANKED)]
        stored = [sem(f"stored{i}") for i in range(2)]

        block = ctx.enter_context(nc.Block())

        @block.sync
        def _(sp):
            sp.dma_start(xin[:, :, :], xT[:, 0:2 * FRAMES].rearrange("p (a n) -> p a n", a=2)).then_inc(s["xin_loaded"], 16)
            sp.dma_start(w_in_sb[:, :, :], w_in).then_inc(s["mixer_weights"], 16)
            sp.dma_start(b_in_sb[:, :], b_in).then_inc(s["mixer_weights"], 16)
            sp.dma_start(b_out_sb[:, :], b_out).then_inc(s["mixer_weights"], 16)
            sp.dma_start(w_out_sb[:, :, :], w_out).then_inc(s["core_loaded"], 16)
            sp.dma_start(core_sb[:, :], core).then_inc(s["core_loaded"], 16)
            sp.dma_start(q_sb[:, :, :], q_w).then_inc(s["attn_weights"], 16)
            sp.dma_start(v_sb[:, :], v_w).then_inc(s["attn_weights"], 16)
            sp.dma_start(gate_sb[:, :], gate_w).then_inc(s["attn_weights"], 16)
            sp.dma_start(w1_sb[:, :], w1).then_inc(s["expert_weights"], 16)
            sp.dma_start(w3_sb[:, :], w3).then_inc(s["expert_weights"], 16)
            sp.dma_start(w2_sb[:, :], w2).then_inc(s["expert_weights"], 16)
            sp.dma_start(sw1_sb[:, :], sw1).then_inc(s["shared_weights"], 16)
            sp.dma_start(sw2_sb[:, :], sw2).then_inc(s["shared_weights"], 16)
            sp.wait_ge(s["filled"], 1)
            sp.dma_start(lists.rearrange("(p n) a -> p (n a)", p=128), no_rows[:, :]).then_inc(s["lists_cleared"], 16)

            def step(it, par):
                a, d = it + 2, it - 1
                nxt = a + 1
                if runs(a) and (not isinstance(nxt, int) or nxt < PAIRS):
                    wait(sp, s["mix_mm"], a * 16 + 2)
                    wait(sp, s["x_squared"], a * 2 + 2)
                    src = xT[:, bass.ds(nxt * (2 * FRAMES), 2 * FRAMES)]
                    sp.dma_start(xin[:, :, :], src.rearrange("p (a n) -> p a n", a=2)).then_inc(s["xin_loaded"], 16)
                if runs(d):
                    wait(sp, s["xn2_ok"], d * RT + RT)
                    dst = row_store[bass.ds(d * COLS, COLS), :].rearrange("(t p) n -> p t n", p=128)
                    sp.dma_start(dst, rows[:, :, :]).then_inc(s["rows_stored"], 16)

            iterations(sp, step)

            sp.wait_ge(s["rows_stored"], 16 * PAIRS)
            sp.wait_ge(s["scattered"], 16 * PAIRS * RT)
            sp.wait_ge(s["table_ok"], 1)

            def load_ids(t, n, turn):
                wait(sp, stored[n % 2], ((turn - 1) * (LISTED // 2) + n // 2 + 1) * 16)
                place_t = sp.value_load(tab_row[0:1, bass.ds(t, 1)], min_val=0, max_val=(E + 1) * CAP_TILES - 1)
                sp.dma_start(tile_ids[n][:, :], lists[bass.ds(place_t * 128, 128), :]).then_inc(ids_in[n], 16)

            tiles(sp, load_ids)
            for par in range(2):
                sp.wait_ge(stored[par], 16 * ((TILES + 1 - par) // 2))

        @block.gpsimd
        def _(gp):
            gp.memset(no_rows[:, :], NO_ROW).then_inc(s["filled"], 1)
            gp.memset(ident[:, :], 0.0).then_inc(s["gp_const"], 1)
            gp.memset(before[:, :], 1.0).then_inc(s["gp_const"], 1)
            gp.memset(valid[:, :], 1.0).then_inc(s["gp_const"], 1)
            gp.memset(valid_hi[:, :], 0.0).then_inc(s["gp_const"], 1)
            gp.iota(ids_f[:, :], pattern=[[128, RT]], base=0, channel_multiplier=1,
                    allow_small_or_imprecise_dtypes=True)
            gp.iota(expert_no[:, :], pattern=[[1, E]], base=0, channel_multiplier=0,
                    allow_small_or_imprecise_dtypes=True)
            gp.iota(next_place[:, :], pattern=[[CAP, E]], base=0, channel_multiplier=0,
                    allow_small_or_imprecise_dtypes=True)
            gp.iota(list_start[:, :], pattern=[[CAP, E]], base=0, channel_multiplier=0,
                    allow_small_or_imprecise_dtypes=True)
            gp.iota(tile_no[:, :], pattern=[[1, TILES]], base=0, channel_multiplier=0,
                    allow_small_or_imprecise_dtypes=True).then_inc(s["gp_const"], 1)
            gp.wait_ge(s["gp_const"], 5)
            gp.affine_select(out=ident[:, :], in_=ident[:, :], compare_op=ALU.not_equal, fill=1.0,
                             base=0, pattern=[[-1, 128]], channel_multiplier=1).then_inc(s["gp_const"], 1)
            gp.affine_select(out=before[:, :], in_=before[:, :], compare_op=ALU.is_gt, fill=0.0,
                             base=0, pattern=[[1, 128]], channel_multiplier=-1).then_inc(s["gp_const"], 1)
            gp.affine_select(out=valid[:, 1:2], in_=valid[:, 1:2], compare_op=ALU.is_ge, fill=0.0,
                             base=M1 - 1, pattern=[[0, 1]], channel_multiplier=-1)
            gp.affine_select(out=valid[:, 2:3], in_=valid[:, 2:3], compare_op=ALU.is_ge, fill=0.0,
                             base=TOK - 64 - 1, pattern=[[0, 1]], channel_multiplier=-1)
            gp.affine_select(out=valid_hi[:, 1:2], in_=valid_hi[:, 1:2], compare_op=ALU.is_gt, fill=1.0,
                             base=64, pattern=[[0, 1]], channel_multiplier=-1).then_inc(s["gp_const"], 1)
            gp.wait_ge(s["dve_const"], 1)

            def step(it, par):
                a, b, d, e = it + 2, it + 1, it - 1, it - 2
                for k in range(HEADS):
                    i = k // 2
                    if k == 2 and runs(b):
                        wait_apart(gp, s["mean1"], b * RT + RT, s["filled"])
                        gp.tensor_scalar(ve1[:, :], mv1[:, :, 1], EPS, None, ALU.add).then_inc(s["var1_eps"], 1)
                        wait(gp, s["var1_eps"], b + 1)
                        gp.tensor_tensor(rstd1[:, :], ve1[:, :], minus_half[:, :], ALU.pow).then_inc(s["rstd1_ok"], 1)
                    if runs(a) and k % 2 == 0:
                        for h in range(2):
                            wait(gp, s["mix_act"], a * 16 + 4 * i + h + 1)
                            gp.tensor_tensor(sq[i][:, h, :], xl[i][:, h, :], xl[i][:, h, :], ALU.mult)\
                              .then_inc(s["squared"], 1)
                    if runs(a) and k == 1:
                        wait(gp, s["xin_loaded"], a * 16 + 16)
                        wait(gp, s["z0_act"], a * 2)
                        for h in range(2):
                            gp.tensor_tensor(x_sq[:, h, :], xin[:, h, :], xin[:, h, :], ALU.mult)\
                              .then_inc(s["x_squared"], 1)
                    if k == 4 and runs(d):
                        wait_apart(gp, s["mean2"], d * RT + RT, s["filled"])
                        gp.tensor_scalar(ve2[:, :], mv2[:, :, 1], EPS, None, ALU.add).then_inc(s["var2_eps"], 1)
                        wait(gp, s["var2_eps"], d + 1)
                        gp.tensor_tensor(rstd2[:, :], ve2[:, :], minus_half[:, :], ALU.pow).then_inc(s["rstd2_ok"], 1)
                    if runs(a) and k in (3, 4, 5, 7):
                        n = (3, 4, 5, 7).index(k)
                        for h in range(2):
                            if k == 4:
                                wait(gp, s["z0_act"], a * 2 + h + 1)
                            else:
                                wait(gp, s["mix_act"], a * 16 + 4 * i + h + 3)
                            if n == 0:
                                wait(gp, s["pooled_ok"], a * 2 + h - 1)
                            else:
                                wait(gp, s["z_added"], a * 8 + 2 * (n - 1) + h + 1)
                            left = z[1] if n == 0 else z_sum
                            right = z[0] if k == 4 else z[i + 1]
                            gp.tensor_tensor(z_sum[:, h, :], left[:, h, :], right[:, h, :], ALU.add)\
                              .then_inc(s["z_added"], 1)
                    if k == 5 and runs(e):
                        wait_apart(gp, s["scattered"], e * RT * 16, s["filled"])
                        wait_apart(gp, s["ids_stepped"], e, s["filled"])
                        gp.tensor_copy(ids[:, :], ids_f[:, :]).then_inc(s["ids_ok"], 1)
                        wait_apart(gp, s["ids_ok"], e + 1, s["filled"])
                        gp.tensor_scalar(ids_f[:, :], ids_f[:, :], float(COLS), None, ALU.add).then_inc(s["ids_stepped"], 1)
                        wait_apart(gp, s["placei_ok"], e + 1, s["filled"])
                        if isinstance(e, int) and e == 0:
                            gp.wait_ge(s["lists_cleared"], 16)
                        for t in range(RT):
                            gp.indirect_dma_start(lists, bass.IndirectOffsetOnAxis(ap=place_i[:, t:t + 1], axis=0),
                                                  ids[:, t:t + 1], None, bounds_check=E * CAP - 1,
                                                  oob_is_err=False).then_inc(s["scattered"], 16)

            iterations(gp, step)

            gp.wait_ge(s["rows_stored"], 16 * PAIRS)

            def gather(t, n, turn):
                if not has(t):
                    return
                wait_apart(gp, ids_in[n % LISTED], (turn + 1 + n // LISTED) * 16, s["filled"])
                wait_apart(gp, s["res_ok"], t - BANKED + 1, s["filled"])
                gp.indirect_dma_start(got[n % BANKED][:, :], None, row_store,
                                      bass.IndirectOffsetOnAxis(ap=tile_ids[n % LISTED][:, :], axis=0),
                                      bounds_check=ROWS - 1, oob_is_err=False).then_inc(got_in[n % BANKED], 16)

            def scatter(t, n, turn):
                gather(t + BANKED, n + BANKED, turn)
                wait_apart(gp, s["res_ok"], t + 1, s["filled"])
                gp.indirect_dma_start(out, bass.IndirectOffsetOnAxis(ap=tile_ids[n][:, :], axis=0),
                                      res[n % 2][:, :], None, bounds_check=ROWS - 1,
                                      oob_is_err=False).then_inc(stored[n % 2], 16)

            for t in range(BANKED):
                gather(t, t, 0)
            tiles(gp, scatter)

        @block.scalar
        def _(act):
            act.wait_ge(s["mixer_weights"], 48)
            act.wait_ge(s["core_loaded"], 32)
            act.activation(core_abs[:, :], core_sb[:, :], ACT.Abs).then_inc(s["core_ready"], 1)
            act.wait_ge(s["core_ready"], 1)

            def mixer_tanh(a, u):
                i, outer, h = u // 4, (u // 2) % 2, u % 2
                wait(act, s["mix_mm"], a * 16 + u + 1)
                if u == 2:
                    wait(act, s["z_added"], a * 8)
                dst = z[i + 1] if outer else xl[i]
                bias = b_out_sb if outer else b_in_sb
                act.activation(dst[:, h, :], mix_ps[:, 0:FRAMES], ACT.Tanh, bias=bias[:, i:i + 1])\
                   .then_inc(s["mix_act"], 1)

            def step(it, par):
                a, b, c, d = it + 2, it + 1, it, it - 1
                for k in range(HEADS):
                    if runs(a):
                        mixer_tanh(a, 2 * k)
                    if runs(c):
                        wait(act, s["max_ok"], c * 8 + k + 1)
                        wait(act, s["pT_tr"], (c * 8 + k - 1) * 2)
                        for t in range(RT):
                            e = act.activation(prob[k % 2][:, t, :], scores[:, t, :], ACT.Exp,
                                               bias=neg_max[:, k % 2, t:t + 1])
                        e.then_inc(s["exp_ok"], 1)
                    if runs(a):
                        mixer_tanh(a, 2 * k + 1)
                        if k == 2:
                            for h in range(2):
                                wait(act, s["x_squared"], a * 2 + h + 1)
                                act.activation(z[0][:, h, :], x_sq[:, h, :], ACT.Tanh, scale=core_abs[:, 0:1])\
                                   .then_inc(s["z0_act"], 1)
                    q, hd = (d, HEADS - 1) if k == 0 else (c, k - 1)
                    if runs(q):
                        wait(act, s["pT_tr"], (q * 8 + hd) * 2 + 2)
                        act.activation(pT1[:, hd, :], pT1_ps[0:M1, 0:COLS], ACT.Copy).then_inc(s["pT1_ok"], 1)
                    if k == 4 and runs(b):
                        wait(act, s["h_out"], b + 1)
                        wait(act, s["h2_ok"], (b - 1) * 2)
                        act.activation(h_res[1 - par][:, :, :], h_raw[:, :, :], ACT.Copy).then_inc(s["h_kept"], 1)

            iterations(act, step)

            def xgT_copy(t, n):
                if has(t):
                    wait(act, s["x_tr"], t + 1)
                    wait(act, s["sh_mm"], t - 1)
                    act.activation(xgT[n % 2][:, :], b_ps[:, 0:128], ACT.Copy).then_inc(s["xgT_ok"], 1)

            def activate(t, n):
                if has(t):
                    wait(act, s["up_mm"], t * 2 + 1)
                    wait(act, s["gate_ok"], t)
                    act.activation(half_tanh[:, :], up_ps[n % 2][:, :], ACT.Tanh, scale=0.5).then_inc(s["tanh_ok"], 1)

            def activate_shared(t, n):
                if has(t):
                    wait(act, s["sh_mm"], t + 1)
                    wait(act, s["down_mm"], t - 1)
                    act.activation(shared[n % 2][:, :], sh_ps[:, :], ACT.Gelu).then_inc(s["gelu_ok"], 1)

            def step2(t, n, turn):
                activate(t + 1, n + 1)
                wait(act, s["hid_tr"], t + 1)
                wait(act, s["down_mm"], t)
                act.activation(hidT[:, :], hidT_ps[:, :], ACT.Copy).then_inc(s["hidT_ok"], 1)
                activate_shared(t + 1, n + 1)
                xgT_copy(t + 2, n)

            xgT_copy(0, 0)
            activate(0, 0)
            activate_shared(0, 0)
            xgT_copy(1, 1)
            tiles(act, step2)

        @block.vector
        def _(dve):
            dve.memset(ones[:, :], 1.0)
            dve.memset(minus_half[:, :], -0.5)
            dve.memset(zero8[:, :], 0.0)
            dve.memset(pooled[:, :], 0.0)
            for p in range(2):
                dve.memset(xv[p][:, :, :, 0:HD], 0.0)
                dve.memset(xv[p][:, :, :, HD:HD + 1], 1.0)
                dve.memset(xv[p][:, :, :, HD + 1:VW], 0.0)
            dve.memset(rden[:, :], 0.0).then_inc(s["dve_const"], 1)
            dve.wait_ge(s["core_ready"], 1)
            dve.wait_ge(s["core_loaded"], 32)
            for i in range(LAYERS):
                w = dve.tensor_scalar(w_out_c[:, i, :], w_out_sb[:, i, :], core_abs[:, i + 1:i + 2], None, ALU.mult)
            w.then_inc(s["core_ready"], 1)
            dve.wait_ge(s["gp_const"], 8)
            dve.tensor_tensor(valid[:, :], valid[:, :], valid_hi[:, :], ALU.add).then_inc(s["dve_const"], 1)
            dve.wait_ge(s["dve_const"], 2)
            dve.tensor_scalar(pad_far[:, :], valid[:, :], -float(NO_ROW), float(NO_ROW), ALU.mult, ALU.add)\
               .then_inc(s["dve_const"], 1)
            dve.wait_ge(s["dve_const"], 3)

            def layernorm(src, st, mv, stat, mean, n):
                for t in range(RT):
                    dve.bn_stats(st[:, t, :], src[t]).then_inc(s[stat], 1)
                for t in range(RT):
                    wait_apart(dve, s[stat], n * RT + t + 1, s["gp_const"])
                    dve.bn_aggr(mv[:, t, :], st[:, t, :]).then_inc(s[mean], 1)

            def merge(pair, g, p):
                tr = d_ps[:, 0:COLS].rearrange("p (n v) -> p n v", v=VW)
                wait(dve, s["oT_tr"], pair * 2 + g + 1)
                dve.reciprocal(rden[:, :], tr[:, :, HD]).then_inc(s["rden_ok"], 1)
                wait(dve, s["rden_ok"], pair * 2 + g + 1)
                dve.tensor_tensor(attn[:, :, :], tr[:, :, 0:HD],
                                  rden[:, :].rearrange("p (n o) -> p n o", o=1).to_broadcast([128, RT * 4, HD]),
                                  ALU.mult).then_inc(s["attn_ok"], 1)
                wait(dve, s["attn_ok"], pair * 2 + g + 1)
                wait(dve, s["h_kept"], pair + 1)
                if g == 0:
                    wait(dve, s["rows_stored"], pair * 16)
                dve.tensor_tensor(rows[:, :, D + 64 * g:D + 64 * g + 64],
                                  h_res[p][:, :, 64 * g:64 * g + 64],
                                  attn[:, :, :].rearrange("p (t h) v -> p t (h v)", t=RT),
                                  ALU.add).then_inc(s["h2_ok"], 1)

            def qx_copy(b, j, p):
                wait(dve, s["qx_mm"], b * 8 + j + 1)
                dve.tensor_copy(qx[p][:, j, :], b_ps[:, 0:COLS]).then_inc(s["qx_ok"], 1)

            def step(it, par):
                b, c, d, e = it + 1, it, it - 1, it - 2
                for k in range(HEADS):
                    if runs(c):
                        wait(dve, s["score_mm"], c * 8 + k + 1)
                        dve.tensor_reduce(neg_max[:, k % 2, :], scores, AX.X, ALU.max, negate=True)\
                           .then_inc(s["max_ok"], 1)
                    if k == 2 and runs(e):
                        wait(dve, s["rank_mm"], e + 1)
                        rank = d_ps[:, 0:RT * E].rearrange("p (t e) -> p t e", t=RT)
                        wait(dve, s["next_ok"], e)
                        dve.tensor_tensor(place[:, :, :], rank,
                                          next_place[:, :].rearrange("p (o e) -> p o e", o=1).to_broadcast([128, RT, E]),
                                          ALU.add).then_inc(s["place_ok"], 1)
                        wait(dve, s["place_ok"], e + 1)
                        dve.tensor_tensor(next_place[:, :], next_place[:, :], d_ps[:, RT * E:RT * E + E],
                                          ALU.add).then_inc(s["next_ok"], 1)
                    if k == 3 and runs(b):
                        wait(dve, s["rstd1_ok"], b + 1)
                        for t in range(RT):
                            dve.tensor_scalar(xn[:, t, :], h_raw[:, t, :], mv1[:, t, 0:1], rstd1[:, t:t + 1],
                                              ALU.subtract, ALU.mult).then_inc(s["xn_ok"], 1)
                    if k == 2 and runs(d):
                        wait(dve, s["pv_mm"], d * 2 + 2)
                        dve.tensor_copy(oT[:, 1, :], pv_ps[:, 0:COLS]).then_inc(s["oT_ok"], 1)
                    if k == 6 and runs(d):
                        wait(dve, s["xn2_tr"], d + 1)
                        dve.tensor_copy(xn2T[:, :], d_ps[:, 0:COLS]).then_inc(s["xn2T_ok"], 1)
                    if k >= 4 and runs(b):
                        qx_copy(b, 2 * (k - 4), 1 - par)
                    if k == 7 and runs(d):
                        wait(dve, s["gate_mm"], d + 1)
                        dve.tensor_copy(logits[:, :, :], d_ps[:, 0:RT * E].rearrange("p (t e) -> p t e", t=RT))\
                           .then_inc(s["logits_ok"], 1)
                    if k == 0 and runs(b):
                        for h in range(2):
                            wait(dve, s["z_added"], b * 8 + 6 + h + 1)
                            if h == 0:
                                wait(dve, s["hT_tr"], b)
                            pairs = z_sum[:, h, :].rearrange("p (n two) -> p n two", two=2)
                            dve.tensor_tensor(pooled[:, h * HALF:h * HALF + TOK], pairs[:, :, 0], pairs[:, :, 1],
                                              ALU.add).then_inc(s["pooled_ok"], 1)
                    if k == 0 and runs(c):
                        wait(dve, s["xv_mm"], c + 1)
                        src = b_ps[:, :].rearrange("p (c h v) -> p c h v", c=4, h=HEADS)
                        dve.tensor_copy(xv[par][:, 0:3:2, :, 0:HD], src[:, 0:3:2, :, :])
                        dve.tensor_copy(xv[par][0:M1, 1:4:2, :, 0:HD], src[0:M1, 1:4:2, :, :]).then_inc(s["xv_ok"], 1)
                    q, hd = (d, HEADS - 1) if k == 0 else (c, k - 1)
                    if runs(q):
                        wait(dve, s["pT_tr"], (q * 8 + hd) * 2 + 1)
                        dve.tensor_copy(pT0[:, hd, :], pT0_ps[:, 0:COLS]).then_inc(s["pT0_ok"], 1)
                    if k >= 4 and runs(b):
                        qx_copy(b, 2 * (k - 4) + 1, 1 - par)
                    if k == 5 and runs(d):
                        wait(dve, s["rstd2_ok"], d + 1)
                        for t in range(RT):
                            dve.tensor_scalar(rows[:, t, 0:D], rows[:, t, D:2 * D], mv2[:, t, 0:1],
                                              rstd2[:, t:t + 1], ALU.subtract, ALU.mult).then_inc(s["xn2_ok"], 1)
                    if k == 0 and runs(d):
                        merge(d, 0, 1 - par)
                    if k == 1 and runs(b):
                        wait(dve, s["hT_tr"], b + 1)
                        wait(dve, s["h_kept"], b)
                        dve.tensor_scalar(h_raw[:, :, :], b_ps[:, 0:COLS].rearrange("p (t n) -> p t n", t=RT),
                                          1.0 / (2 * (LAYERS + 1)), None, ALU.mult).then_inc(s["h_out"], 1)
                        wait(dve, s["h_out"], b + 1)
                        layernorm([h_raw[:, t, :] for t in range(RT)], st1, mv1, "stat1", "mean1", b)
                    if k == 2:
                        if runs(e):
                            dve.tensor_tensor(place_of[:, :, :], place[:, :, :], chosen[:, :, :], ALU.mult)\
                               .then_inc(s["placeof_ok"], 1)
                            wait(dve, s["placeof_ok"], e + 1)
                            dve.tensor_reduce(place_f[:, :], place_of[:, :, :], AX.X, ALU.add).then_inc(s["placef_ok"], 1)
                            wait(dve, s["placef_ok"], e + 1)
                            wait(dve, s["scattered"], e * RT * 16)
                            dve.tensor_tensor(place_i[:, :], place_f[:, :], pad_far[:, :], ALU.add)\
                               .then_inc(s["placei_ok"], 1)
                    if k == 3:
                        if runs(d):
                            merge(d, 1, 1 - par)
                        if runs(b):
                            wait(dve, s["xn_tr"], b + 1)
                            dve.tensor_copy(xnT[1 - par][:, :], b_ps[:, 0:COLS]).then_inc(s["xnT_ok"], 1)
                        if runs(d):
                            wait(dve, s["h2_ok"], d * 2 + 2)
                            layernorm([rows[:, t, D:2 * D] for t in range(RT)], st2, mv2, "stat2", "mean2", d)
                    if k == 6:
                        if runs(c):
                            wait(dve, s["pv_mm"], c * 2 + 1)
                            dve.tensor_copy(oT[:, 0, :], pv_ps[:, 0:COLS]).then_inc(s["oT_ok"], 1)
                    if k == 7 and runs(d):
                        wait_apart(dve, s["logits_ok"], d + 1, s["gp_const"])
                        for t in range(RT):
                            dve.max(top[:, t, :], logits[:, t, :]).then_inc(s["top_ok"], 1)
                        for t in range(RT):
                            wait_apart(dve, s["top_ok"], d * RT + t + 1, s["gp_const"])
                            dve.max_index(top_i[:, t, :], top[:, t, :], logits[:, t, :]).then_inc(s["topi_ok"], 1)
                        wait(dve, s["topi_ok"], d * RT + RT)
                        dve.tensor_copy(top_f[:, :], top_i[:, :, 0]).then_inc(s["topf_ok"], 1)
                        wait(dve, s["topf_ok"], d + 1)
                        dve.tensor_tensor(is_top[:, :, :],
                                          expert_no[:, :].rearrange("p (o e) -> p o e", o=1).to_broadcast([128, RT, E]),
                                          top_f[:, :].rearrange("p (t o) -> p t o", o=1).to_broadcast([128, RT, E]),
                                          ALU.is_equal).then_inc(s["istop_ok"], 1)
                        wait(dve, s["istop_ok"], d + 1)
                        dve.tensor_tensor(chosen[:, :, :], is_top[:, :, :],
                                          valid[:, :].rearrange("p (t o) -> p t o", o=1).to_broadcast([128, RT, E]),
                                          ALU.mult).then_inc(s["chosen_ok"], 1)

            iterations(dve, step)

            n = 0

            def done(ins):
                nonlocal n
                n += 1
                ins.then_inc(s["table_step"], 1)
                dve.wait_ge(s["table_step"], n)

            def over_tiles(ap):
                return ap.rearrange("p (o e) -> p o e", o=1).to_broadcast([1, TILES, E])

            dve.wait_ge(s["next_ok"], PAIRS)
            done(dve.tensor_tensor(count[:, :], next_place[0:1, :], list_start[:, :], ALU.subtract))
            done(dve.tensor_scalar(count_i[:, :], count[:, :], 127.0, None, ALU.add))
            done(dve.tensor_scalar(ntile_i[:, :], count_i[:, :], 7, None, ALU.arith_shift_right))
            done(dve.tensor_copy(ntile[:, :], ntile_i[:, :]))
            done(dve.tensor_tensor_scan(ends[:, :], ntile[:, :], zero8[:, :], 0.0, ALU.add, ALU.add))
            done(dve.tensor_tensor(past[:, :, :],
                                   tile_no[:, :].rearrange("p (t o) -> p t o", o=1).to_broadcast([1, TILES, E]),
                                   over_tiles(ends[:, :]), ALU.is_ge))
            done(dve.tensor_reduce(t_exp[:, :], past[:, :, :], AX.X, ALU.add))
            done(dve.tensor_tensor(past_n[:, :, :], past[:, :, :], over_tiles(ntile[:, :]), ALU.mult))
            done(dve.tensor_reduce(t_skip[:, :], past_n[:, :, :], AX.X, ALU.add))
            done(dve.tensor_tensor(t_row[:, :], tile_no[:, :], t_skip[:, :], ALU.subtract))
            done(dve.tensor_scalar(t_row2[:, :], t_exp[:, :], float(CAP_TILES), None, ALU.mult))
            done(dve.tensor_tensor(tab_row[:, :], t_row2[:, :], t_row[:, :], ALU.add))
            dve.tensor_scalar(tab_w[:, :], t_exp[:, :], float(E - 1), float(INNER), ALU.min, ALU.mult)\
               .then_inc(s["table_ok"], 1)

            def hidden(t, n):
                if not has(t):
                    return
                wait(dve, s["hid_ok"], t)
                wait(dve, s["tanh_ok"], t + 1)
                dve.scalar_tensor_tensor(gate_u[:, :], half_tanh[:, :], 1.0, up_ps[n % 2][:, :], ALU.add, ALU.mult)\
                   .then_inc(s["gate_ok"], 1)
                wait(dve, s["gate_ok"], t + 1)
                wait(dve, s["up_mm"], t * 2 + 2)
                wait(dve, s["hid_tr"], t - 1)
                dve.scalar_tensor_tensor(hid[n % 2][:, :], gate_u[:, :], 0.5, up_ps[2 + n % 2][:, :], ALU.mult, ALU.mult)\
                   .then_inc(s["hid_ok"], 1)

            def step2(t, n, turn):
                hidden(t + 1, n + 1)
                wait(dve, stored[n % 2], (turn * (LISTED // 2) + n // 2) * 16)
                wait(dve, s["down_mm"], t + 1)
                dve.tensor_tensor(res[n % 2][:, :], got[n % BANKED][:, D:2 * D], y_ps[:, 0:D], ALU.add)\
                   .then_inc(s["res_ok"], 1)

            hidden(0, 0)
            tiles(dve, step2)

        @block.tensor
        def _(pe):
            pe.wait_ge(s["mixer_weights"], 48)
            pe.wait_ge(s["core_ready"], 2)
            pe.wait_ge(s["gp_const"], 8)

            def mixer(a, u):
                i, outer, h = u // 4, (u // 2) % 2, u % 2
                wait(pe, s["mix_act"], a * 16 + u)
                if outer:
                    wait(pe, s["squared"], a * 8 + 2 * i + h + 1)
                    w, rhs = w_out_c, sq[i]
                else:
                    if i == 0:
                        wait(pe, s["xin_loaded"], a * 16 + 16)
                    w, rhs = w_in_sb, (xin if i == 0 else xl[i - 1])
                pe.matmul(mix_ps[:, 0:FRAMES], w[:, i, :], rhs[:, h, :], start=True, stop=True)\
                  .then_inc(s["mix_mm"], 1)

            def three_transposes(dst, src, done):
                for t in range(RT):
                    tr = pe.transpose(dst(t), src(t), ident[:, :])
                tr.then_inc(done, 1)

            def b_piece(b, k, p, late):
                if k == 0 and late:
                    wait(pe, s["pooled_ok"], b * 2 + 2)
                    wait(pe, s["xv_ok"], b)
                    three_transposes(lambda t: b_ps[:, t * 128:t * 128 + 128],
                                     lambda t: pooled[:, t * 128:t * 128 + 128], s["hT_tr"])
                if k == 3 and late:
                    wait(pe, s["xn_ok"], b * RT + RT)
                    three_transposes(lambda t: b_ps[:, t * 128:t * 128 + 128],
                                     lambda t: xn[:, t, :], s["xn_tr"])
                if k >= 4:
                    j = 2 * (k - 4) + late
                    if j == 0:
                        wait(pe, s["xnT_ok"], b + 1)
                        if isinstance(b, int) and b == 0:
                            pe.wait_ge(s["attn_weights"], 48)
                    else:
                        wait(pe, s["qx_ok"], b * 8 + j)
                    pe.matmul(b_ps[:, 0:COLS], q_sb[:, j, :], xnT[p][:, :], start=True, stop=True)\
                      .then_inc(s["qx_mm"], 1)

            def values(c, p):
                wait(pe, s["qx_ok"], c * 8 + 8)
                for c4, (m0, m) in enumerate(((0, 128), (128, M1), (HALF, 128), (HALF + 128, M1))):
                    v = pe.matmul(b_ps[0:m, c4 * 128:c4 * 128 + 128], xnT[p][:, m0:m0 + m], v_sb[:, :],
                                  start=True, stop=True)
                v.then_inc(s["xv_mm"], 1)

            def scores_of(c, h, p):
                if h == 0:
                    wait(pe, s["qx_ok"], c * 8 + 8)
                wait(pe, s["exp_ok"], c * 8 + h)
                qh, keys = qx[p][:, h, :], (xnT[p][:, 0:TOK], xnT[p][:, HALF:HALF + TOK])
                pe.matmul(scores[:, 0, :], qh[:, 0:128], keys[0], start=True, stop=True)
                pe.matmul(scores[:, 2, :], qh[:, 256:384], keys[1], start=True, stop=True)
                pe.matmul(scores[0:64, 1, :], qh[:, 128:192], keys[0], start=True, stop=True)
                pe.matmul(scores[64:128, 1, :], qh[:, 192:256], keys[1], start=True, stop=True)\
                  .then_inc(s["score_mm"], 1)

            def probs_T(q, h):
                wait(pe, s["exp_ok"], q * 8 + h + 1)
                wait(pe, s["pT0_ok"], q * 8 + h)
                three_transposes(lambda t: pT0_ps[:, t * 128:t * 128 + 128],
                                 lambda t: prob[h % 2][:, t, 0:128], s["pT_tr"])
                wait_apart(pe, s["pT1_ok"], q * 8 + h, s["gp_const"])
                three_transposes(lambda t: pT1_ps[0:M1, t * 128:t * 128 + 128],
                                 lambda t: prob[h % 2][:, t, 128:TOK], s["pT_tr"])

            def weighted(q, g, p):
                wait(pe, s["xv_ok"], q + 1)
                wait(pe, s["pT0_ok"], q * 8 + 4 * g + 4)
                wait(pe, s["pT1_ok"], q * 8 + 4 * g + 4)
                wait(pe, s["oT_ok"], q * 2 + g)
                for half in range(2):
                    cols = slice(half * HALF, half * HALF + HALF)
                    for chunk, (m, src) in enumerate(((128, pT0), (M1, pT1))):
                        for j in range(4):
                            h = 4 * g + j
                            v = pe.matmul(pv_ps[32 * j:32 * j + VW, cols], xv[p][0:m, 2 * half + chunk, h, :],
                                          src[0:m, h, cols], start=(chunk == 0), stop=(chunk == 1))
                v.then_inc(s["pv_mm"], 1)

            def heads_T(q, g):
                wait(pe, s["oT_ok"], q * 2 + g + 1)
                three_transposes(lambda t: d_ps[:, t * 128:t * 128 + 128],
                                 lambda t: oT[:, g, t * 128:t * 128 + 128], s["oT_tr"])

            def rank(e):
                wait(pe, s["chosen_ok"], e + 1)
                wait(pe, s["attn_ok"], e * 2 + 3 if not isinstance(e, int) or e + 1 < PAIRS else e * 2 + 2)
                for t in range(RT):
                    for t2 in range(t):
                        pe.matmul(d_ps[:, t * E:t * E + E], ones[:, :], chosen[:, t2, :],
                                  start=(t2 == 0), stop=False)
                    pe.matmul(d_ps[:, t * E:t * E + E], before[:, :], chosen[:, t, :],
                              start=(t == 0), stop=True)
                for t in range(RT):
                    m = pe.matmul(d_ps[:, RT * E:RT * E + E], ones[:, :], chosen[:, t, :],
                                  start=(t == 0), stop=(t == RT - 1))
                m.then_inc(s["rank_mm"], 1)

            def late_unit(it, k, p):
                a, b = it + 2, it + 1
                if runs(b) and k > 0:
                    b_piece(b, k, p, 1)
                if runs(a):
                    mixer(a, 2 * k + 1)
                if runs(b) and k == 0:
                    b_piece(b, k, p, 1)

            def step(it, par):
                a, b, c, d, e = it + 2, it + 1, it, it - 1, it - 2
                for k in range(HEADS):
                    if runs(c):
                        scores_of(c, k, par)
                    if k == 3 and runs(d):
                        wait(pe, s["next_ok"], d)
                        heads_T(d, 1)
                    if runs(b):
                        b_piece(b, k, 1 - par, 0)
                    if runs(a):
                        mixer(a, 2 * k)
                    if k == 0 and runs(c):
                        values(c, par)
                    q, h = (d, HEADS - 1) if k == 0 else (c, k - 1)
                    if runs(q):
                        probs_T(q, h)
                    if k in (0, 4, 5, 6, 7):
                        late_unit(it, k, 1 - par)
                    if k == 1 and runs(e):
                        rank(e)
                    if k == 1 and runs(d):
                        weighted(d, 1, 1 - par)
                    if k in (1, 2, 3):
                        late_unit(it, k, 1 - par)
                    if k == 5 and runs(c):
                        weighted(c, 0, par)
                    if k == 5 and runs(d):
                        wait(pe, s["xn2_ok"], d * RT + RT)
                        three_transposes(lambda t: d_ps[:, t * 128:t * 128 + 128],
                                         lambda t: rows[:, t, 0:D], s["xn2_tr"])
                    if k == 6 and runs(d):
                        wait(pe, s["xn2T_ok"], d + 1)
                        for t in range(RT):
                            g = pe.matmul(d_ps[:, t * E:t * E + E], xn2T[:, t * 128:t * 128 + 128],
                                          gate_sb[:, :], start=True, stop=True)
                        g.then_inc(s["gate_mm"], 1)
                    if k == 7 and runs(c):
                        if runs(d):
                            wait(pe, s["logits_ok"], d + 1)
                        heads_T(c, 0)

            iterations(pe, step)

            pe.wait_ge(s["expert_weights"], 48)
            pe.wait_ge(s["shared_weights"], 32)
            pe.wait_ge(s["table_ok"], 1)

            def expert(t):
                return pe.value_load(tab_w[0:1, bass.ds(t, 1)], min_val=0, max_val=(E - 1) * INNER)

            def rows_T(t, n, turn):
                if has(t):
                    pe.wait_ge(got_in[n % BANKED], (turn * (LISTED // BANKED) + n // BANKED + 1) * 16)
                    wait(pe, s["xgT_ok"], t)
                    pe.transpose(b_ps[:, 0:128], got[n % BANKED][:, 0:D], ident[:, :]).then_inc(s["x_tr"], 1)

            def up(t, n):
                if not has(t):
                    return
                w = expert(t)
                wait(pe, s["xgT_ok"], t + 1)
                wait(pe, s["hid_ok"], t - 1)
                for i, w_sb in enumerate((w1_sb, w3_sb)):
                    pe.matmul(up_ps[2 * i + n % 2][:, :], xgT[n % 2][:, :], w_sb[:, bass.ds(w, INNER)],
                              start=True, stop=True).then_inc(s["up_mm"], 1)

            def up_shared(t, n):
                if not has(t):
                    return
                wait(pe, s["gelu_ok"], t)
                for c in range(NC):
                    m = pe.matmul(sh_ps[:, c * 128:c * 128 + 128], sw1_sb[:, c * 128:c * 128 + 128],
                                  xgT[n % 2][:, :], start=True, stop=True)
                m.then_inc(s["sh_mm"], 1)

            def step2(t, n, turn):
                up(t + 1, n + 1)
                wait(pe, s["hid_ok"], t + 1)
                wait_apart(pe, s["hidT_ok"], t, s["table_ok"])
                for c in range(NC):
                    tr = pe.transpose(hidT_ps[:, c * 128:c * 128 + 128], hid[n % 2][:, c * 128:c * 128 + 128],
                                      ident[:, :])
                tr.then_inc(s["hid_tr"], 1)
                up_shared(t + 1, n + 1)
                rows_T(t + 2, n + 2, turn)
                w = expert(t)
                wait(pe, s["gelu_ok"], t + 1)
                wait(pe, s["res_ok"], t)
                for c in range(NC):
                    pe.matmul(y_ps[:, 0:D], shared[n % 2][:, c * 128:c * 128 + 128],
                              sw2_sb[:, c * 128:c * 128 + 128], start=(c == 0), stop=False)
                wait(pe, s["hidT_ok"], t + 1)
                for c in range(NC):
                    m = pe.matmul(y_ps[:, 0:D], hidT[:, c * 128:c * 128 + 128],
                                  w2_sb[:, bass.ds(w + c * 128, 128)], start=False, stop=(c == NC - 1))
                m.then_inc(s["down_mm"], 1)

            rows_T(0, 0, 0)
            up(0, 0)
            up_shared(0, 0)
            rows_T(1, 1, 0)
            tiles(pe, step2)


def kernel(**inputs):
    import numpy as np
    import concourse.bacc as bacc
    from concourse.bass_utils import run_bass_kernel_spmd

    def lay(name, *order):
        return np.asarray(inputs[name]).transpose(order)

    x = np.asarray(inputs["x"])[:, :FRAMES, :]
    arrays = {
        "xT": x.transpose(2, 0, 1).reshape(D, BATCH * FRAMES),
        "w_in": lay("L0_tok_W_in", 1, 0, 2),
        "b_in": lay("L0_tok_b_in", 1, 0),
        "w_out": lay("L0_tok_W_out", 1, 0, 2),
        "b_out": lay("L0_tok_b_out", 1, 0),
        "core": lay("L0_tok_core_diag", 1, 0),
        "q_w": lay("L0_attn_Q", 1, 0, 2),
        "v_w": lay("L0_attn_V", 1, 0, 2).reshape(D, HEADS * HD),
        "gate_w": lay("L0_ffn_gate_w", 1, 0),
        "w1": lay("L0_ffn_w1", 2, 0, 1).reshape(D, E * INNER),
        "w3": lay("L0_ffn_w3", 2, 0, 1).reshape(D, E * INNER),
        "w2": np.asarray(inputs["L0_ffn_w2"]).reshape(E, D, NC, 128).transpose(3, 0, 2, 1).reshape(128, E * INNER),
        "sw1": lay("L0_ffn_sw1", 1, 0),
        "sw2": np.asarray(inputs["L0_ffn_sw2"]).reshape(D, NC, 128).transpose(2, 1, 0).reshape(128, INNER),
    }
    nc = bacc.Bacc("TRN2", target_bir_lowering=False, num_devices=1)
    feed, args = {}, []
    for name, a in arrays.items():
        a = np.ascontiguousarray(a)
        feed[f"in_{name}"] = a
        args.append(nc.dram_tensor(f"in_{name}", a.shape, mybir.dt.from_np(a.dtype), kind="ExternalInput").ap())
    args.append(nc.dram_tensor("out_rows", (ROWS, D), F32, kind="ExternalOutput").ap())
    tower(nc, *args)
    r = run_bass_kernel_spmd(nc, [feed], core_ids=[0])
    rows = r.results[0]["out_rows"].reshape(BATCH, HALF, D)
    return rows[:, :TOK, :]
```

```python
from contextlib import ExitStack

import concourse.bass as bass
from concourse import mybir

F32 = mybir.dt.float32
BF16 = mybir.dt.bfloat16
I32 = mybir.dt.int32
U32 = mybir.dt.uint32
ALU = mybir.AluOpType
ACT = mybir.ActivationFunctionType
AX = mybir.AxisListType

D = 128
BATCH = 64
FRAMES = 374
TOK = FRAMES // 2
PAIRS = BATCH // 2
HALF = 192
COLS = 2 * HALF
RT = COLS // 128
M1 = TOK - 128
LAYERS = 4
HEADS = 8
HD = 16
VW = 32
E = 8
INNER = 512
NC = INNER // 128
TOKENS = BATCH * TOK
CAP_TILES = -(-TOKENS // 128)
CAP = CAP_TILES * 128
TILES = (TOKENS + E * 127) // 128
ROWS = PAIRS * COLS
NO_ROW = 1 << 20
EPS = 1e-5
FIRST_FULL, LAST_FULL = 4, PAIRS - 4
BANKED = 4
LISTED = 8


def wait(eng, sem, count):
    if not (isinstance(count, int) and count <= 0):
        eng.wait_ge(sem, count)


def wait_apart(eng, sem, count, met):
    if not isinstance(count, int):
        count = eng.to_reg(count)
        eng.wait_ge(met, 1)
    wait(eng, sem, count)


def iterations(eng, step):
    for it in range(-2, FIRST_FULL):
        step(it, it % 2)
    turns = (LAST_FULL - FIRST_FULL + 1) // 2
    with eng.Fori(0, turns) as turn:
        step(turn * 2 + FIRST_FULL, FIRST_FULL % 2)
        step(turn * 2 + (FIRST_FULL + 1), (FIRST_FULL + 1) % 2)
    for it in range(FIRST_FULL + 2 * turns, PAIRS + 2):
        step(it, it % 2)


def tiles(eng, step, ready=None):
    for t in range(LISTED):
        step(t, t, 0)
    if ready:
        ready()
    with eng.Fori(1, TILES // LISTED - 1) as turn:
        for n in range(LISTED):
            step(turn * LISTED + n, n, turn)
    for t in range((TILES // LISTED - 1) * LISTED, TILES):
        step(t, t % LISTED, t // LISTED)


def has(tile):
    return not isinstance(tile, int) or 0 <= tile < TILES


def runs(pair):
    return not isinstance(pair, int) or 0 <= pair < PAIRS


def tower(nc, xT, w_in, b_in, w_out, b_out, core, q_w, v_w, gate_w, w1, w3, w2, sw1, sw2, out):
    ctx = ExitStack()
    with ctx:
        def sb(name, shape, dt=F32):
            return ctx.enter_context(nc.sbuf_tensor(name, shape, dt))

        def sem(name):
            return ctx.enter_context(nc.semaphore(name))

        w_in_sb = sb("w_in_sb", [128, LAYERS, D])
        w_out_sb = sb("w_out_sb", [128, LAYERS, D])
        w_out_c = sb("w_out_c", [128, LAYERS, D])
        b_in_sb = sb("b_in_sb", [128, LAYERS])
        b_out_sb = sb("b_out_sb", [128, LAYERS])
        core_sb = sb("core_sb", [128, LAYERS + 1])
        core_abs = sb("core_abs", [128, LAYERS + 1])
        q_sb = sb("q_sb", [128, HEADS, D])
        v_sb = sb("v_sb", [128, HEADS * HD])
        gate_sb = sb("gate_sb", [128, E])
        w1_sb = sb("w1_sb", [128, E * INNER])
        w3_sb = sb("w3_sb", [128, E * INNER])
        w2_sb = sb("w2_sb", [128, E * INNER])
        sw1_sb = sb("sw1_sb", [128, INNER])
        sw2_sb = sb("sw2_sb", [128, INNER])
        ident = sb("ident", [128, 128])
        before = sb("before", [128, 128], BF16)
        ones = sb("ones", [128, 128], BF16)
        minus_half = sb("minus_half", [128, RT])
        expert_no = sb("expert_no", [128, E])
        valid_hi = sb("valid_hi", [128, RT])
        valid = sb("valid", [128, RT])
        pad_far = sb("pad_far", [128, RT])
        xin = sb("xin", [128, 2, FRAMES])
        x_sq = sb("x_sq", [128, 2, FRAMES])
        xl = [sb(f"xl{i}", [128, 2, FRAMES]) for i in range(LAYERS)]
        sq = [sb(f"sq{i}", [128, 2, FRAMES]) for i in range(LAYERS)]
        z = [sb(f"z{i}", [128, 2, FRAMES]) for i in range(LAYERS + 1)]
        z_sum = sb("z_sum", [128, 2, FRAMES])
        pooled = sb("pooled", [128, COLS])
        h_raw = sb("h_raw", [128, RT, D])
        h_res = [sb(f"h_res{i}", [128, RT, D]) for i in range(2)]
        st1 = sb("st1", [128, RT, 6])
        mv1 = sb("mv1", [128, RT, 2])
        ve1 = sb("ve1", [128, RT])
        rstd1 = sb("rstd1", [128, RT])
        xn = sb("xn", [128, RT, D])
        xnT = [sb(f"xnT{i}", [128, COLS]) for i in range(2)]
        qx = [sb(f"qx{i}", [128, HEADS, COLS]) for i in range(2)]
        xv = [sb(f"xv{i}", [128, 4, HEADS, VW]) for i in range(2)]
        neg_max = sb("neg_max", [128, 2, RT])
        prob = [sb(f"prob{i}", [128, RT, 384]) for i in range(2)]
        pT0 = sb("pT0", [128, HEADS, COLS])
        pT1 = sb("pT1", [128, HEADS // 2, COLS])
        oT = sb("oT", [128, 2, COLS])
        rden = sb("rden", [128, RT * 4])
        attn = sb("attn", [128, RT * 4, HD])
        rows = sb("rows", [128, RT, 2 * D])
        st2 = sb("st2", [128, RT, 6])
        mv2 = sb("mv2", [128, RT, 2])
        ve2 = sb("ve2", [128, RT])
        rstd2 = sb("rstd2", [128, RT])
        xn2T = sb("xn2T", [128, COLS])
        logits = sb("logits", [128, RT, E])
        top = sb("top", [128, RT, 8])
        top_i = sb("top_i", [128, RT, 8], U32)
        top_f = sb("top_f", [128, RT])
        is_top = sb("is_top", [128, RT, E])
        chosen = sb("chosen", [128, RT, E], BF16)
        place = sb("place", [128, RT, E])
        place_of = sb("place_of", [128, RT, E])
        place_f = sb("place_f", [128, RT])
        place_i = sb("place_i", [128, RT], I32)
        next_place = sb("next_place", [128, E])
        ids_f = sb("ids_f", [128, RT])
        ids = sb("ids", [128, RT], I32)
        no_rows = sb("no_rows", [128, (E + 1) * CAP // 128], I32)
        count_i = sb("count_i", [1, E], I32)
        ntile_i = sb("ntile_i", [1, E], I32)
        ntile = sb("ntile", [1, E])
        zero8 = sb("zero8", [1, E])
        list_start = sb("list_start", [1, E])
        count = sb("count", [1, E])
        ends = sb("ends", [1, E])
        tile_no = sb("tile_no", [1, TILES])
        past = sb("past", [1, TILES, E])
        past_n = sb("past_n", [1, TILES, E])
        t_exp = sb("t_exp", [1, TILES])
        t_skip = sb("t_skip", [1, TILES])
        t_row = sb("t_row", [1, TILES])
        t_row2 = sb("t_row2", [1, TILES])
        tab_row = sb("tab_row", [1, TILES], I32)
        tab_w = sb("tab_w", [1, TILES], I32)
        tile_ids = [sb(f"tile_ids{i}", [128, 1], I32) for i in range(LISTED)]
        got = [z[i][:, :, :].rearrange("p a n -> p (a n)")[:, 0:2 * D] for i in range(BANKED)]
        xgT = [xn[:, i, :] for i in range(2)]
        res = [h_raw[:, i, :] for i in range(2)]
        half_tanh, gate_u, hidT, *double = (
            m[:, :, :].rearrange("p a n -> p (a n)")[:, 0:INNER] for m in (*sq, *xl[0:3]))
        hid, shared = double[0:2], double[2:4]

        bank = [ctx.enter_context(nc.psum_tensor(f"bank{i}", [128, 512], F32)) for i in range(4)]
        score_ps = ctx.enter_context(nc.psum_tensor("score_ps", [128, 1024], F32))
        side_ps = ctx.enter_context(nc.psum_tensor("side_ps", [128, 1024], F32))
        pT0_ps, pT1_ps, pv_ps, d_ps = bank
        mix_ps, b_ps = side_ps[:, 0:512], side_ps[:, 512:1024]
        up_ps = (pT0_ps, pT1_ps, score_ps[:, 0:512], score_ps[:, 512:1024])
        sh_ps, hidT_ps, y_ps = pv_ps, mix_ps, d_ps

        def mix_bank(a, u):
            return pT0_ps if isinstance(a, int) and a < 2 and u % 2 else mix_ps

        def mix_free(a, u):
            return a * 16 + u - (1 if isinstance(a, int) and a < 2 and u > 0 else 0)

        def scores_in(c, h):
            ps = side_ps if isinstance(c, int) and c == PAIRS - 1 and h % 2 else score_ps
            return ps[:, 0:RT * 256].rearrange("p (t n) -> p t n", t=RT)[:, :, 0:TOK]

        def scores_free(c, h):
            return c * 8 + h - (1 if isinstance(c, int) and c == PAIRS - 1 and h > 0 else 0)

        lists = nc.dram_tensor("lists", ((E + 1) * CAP, 1), I32, kind="Internal").ap()
        row_store = nc.dram_tensor("row_store", (ROWS, 2 * D), F32, kind="Internal").ap()

        s = {n: sem(n) for n in (
            "mixer_weights", "biases", "core_loaded", "attn_weights", "expert_weights", "shared_weights",
            "filled", "lists_cleared",
            "gp_const", "dve_const", "core_ready",
            "xin_loaded", "x_squared", "mix_mm", "mix_act", "z0_act", "squared", "z_added", "pooled_ok",
            "hT_tr", "h_out", "stat1", "mean1", "var1_eps", "rstd1_ok", "xn_ok", "xn_tr", "xnT_ok",
            "qx_mm", "qx_ok", "xv_mm", "xv_ok", "h_kept",
            "score_mm", "max_ok", "exp_ok", "pT_tr", "tail_tr", "pT0_ok", "pT1_ok", "pv_mm", "oT_ok", "oT_tr",
            "rden_ok", "attn_ok", "h2_ok", "stat2", "mean2", "var2_eps", "rstd2_ok", "xn2_ok",
            "rows_stored", "xn2_tr", "xn2T_ok", "gate_mm", "logits_ok", "top_ok", "topi_ok", "topf_ok",
            "istop_ok", "chosen_ok", "rank_mm", "place_ok", "placeof_ok", "placef_ok", "placei_ok",
            "next_ok", "ids_stepped", "ids_ok", "scattered",
            "table_step", "table_ok",
            "up_mm", "sh_mm", "x_tr", "xgT_ok", "tanh_ok", "gelu_ok", "gate_ok", "hid_ok", "hid_tr",
            "hidT_ok", "down_mm", "res_ok")}
        ids_in = [sem(f"ids_in{i}") for i in range(LISTED)]
        got_in = [sem(f"got_in{i}") for i in range(BANKED)]
        stored = [sem(f"stored{i}") for i in range(2)]

        block = ctx.enter_context(nc.Block())

        @block.sync
        def _(sp):
            sp.dma_start(w_in_sb[:, :, :], w_in).then_inc(s["mixer_weights"], 16)
            sp.dma_start(xin[:, :, :], xT[:, 0:2 * FRAMES].rearrange("p (a n) -> p a n", a=2)).then_inc(s["xin_loaded"], 16)
            sp.dma_start(q_sb[:, :, :], q_w).then_inc(s["attn_weights"], 16)
            sp.dma_start(v_sb[:, :], v_w).then_inc(s["attn_weights"], 16)
            sp.dma_start(gate_sb[:, :], gate_w).then_inc(s["attn_weights"], 16)
            sp.dma_start(w1_sb[:, :], w1).then_inc(s["expert_weights"], 16)
            sp.dma_start(w3_sb[:, :], w3).then_inc(s["expert_weights"], 16)
            sp.dma_start(w2_sb[:, :], w2).then_inc(s["expert_weights"], 16)
            sp.dma_start(sw1_sb[:, :], sw1).then_inc(s["shared_weights"], 16)
            sp.dma_start(sw2_sb[:, :], sw2).then_inc(s["shared_weights"], 16)
            sp.wait_ge(s["filled"], 1)
            sp.dma_start(lists.rearrange("(p n) a -> p (n a)", p=128), no_rows[:, :]).then_inc(s["lists_cleared"], 16)

            def step(it, par):
                a, d = it + 2, it - 1
                nxt = a + 1
                if runs(a) and (not isinstance(nxt, int) or nxt < PAIRS):
                    wait(sp, s["mix_mm"], a * 16 + 2)
                    wait(sp, s["x_squared"], a * 2 + 2)
                    src = xT[:, bass.ds(nxt * (2 * FRAMES), 2 * FRAMES)]
                    sp.dma_start(xin[:, :, :], src.rearrange("p (a n) -> p a n", a=2)).then_inc(s["xin_loaded"], 16)
                if runs(d):
                    wait(sp, s["xn2_ok"], d * RT + RT)
                    dst = row_store[bass.ds(d * COLS, COLS), :].rearrange("(t p) n -> p t n", p=128)
                    sp.dma_start(dst, rows[:, :, :]).then_inc(s["rows_stored"], 16)

            iterations(sp, step)

            sp.wait_ge(s["rows_stored"], 16 * PAIRS)
            sp.wait_ge(s["scattered"], 16 * PAIRS * RT)
            sp.wait_ge(s["table_ok"], 1)

            def load_ids(t, n, turn):
                wait(sp, stored[n % 2], ((turn - 1) * (LISTED // 2) + n // 2 + 1) * 16)
                place_t = sp.value_load(tab_row[0:1, bass.ds(t, 1)], min_val=0, max_val=(E + 1) * CAP_TILES - 1)
                sp.dma_start(tile_ids[n][:, :], lists[bass.ds(place_t * 128, 128), :]).then_inc(ids_in[n], 16)

            tiles(sp, load_ids, ready=lambda: sp.wait_ge(s["table_ok"], 4))
            for par in range(2):
                sp.wait_ge(stored[par], 16 * ((TILES + 1 - par) // 2))

        @block.gpsimd
        def _(gp):
            gp.memset(no_rows[:, :], NO_ROW).then_inc(s["filled"], 1)
            gp.memset(ident[:, :], 0.0).then_inc(s["gp_const"], 1)
            gp.memset(before[:, :], 1.0).then_inc(s["gp_const"], 1)
            gp.memset(valid[:, :], 1.0).then_inc(s["gp_const"], 1)
            gp.memset(valid_hi[:, :], 0.0).then_inc(s["gp_const"], 1)
            gp.iota(ids_f[:, :], pattern=[[128, RT]], base=0, channel_multiplier=1,
                    allow_small_or_imprecise_dtypes=True)
            gp.iota(expert_no[:, :], pattern=[[1, E]], base=0, channel_multiplier=0,
                    allow_small_or_imprecise_dtypes=True)
            gp.iota(next_place[:, :], pattern=[[CAP, E]], base=0, channel_multiplier=0,
                    allow_small_or_imprecise_dtypes=True)
            gp.iota(list_start[:, :], pattern=[[CAP, E]], base=0, channel_multiplier=0,
                    allow_small_or_imprecise_dtypes=True)
            gp.iota(tile_no[:, :], pattern=[[1, TILES]], base=0, channel_multiplier=0,
                    allow_small_or_imprecise_dtypes=True).then_inc(s["gp_const"], 1)
            gp.wait_ge(s["gp_const"], 5)
            gp.affine_select(out=ident[:, :], in_=ident[:, :], compare_op=ALU.not_equal, fill=1.0,
                             base=0, pattern=[[-1, 128]], channel_multiplier=1).then_inc(s["gp_const"], 1)
            gp.affine_select(out=before[:, :], in_=before[:, :], compare_op=ALU.is_gt, fill=0.0,
                             base=0, pattern=[[1, 128]], channel_multiplier=-1).then_inc(s["gp_const"], 1)
            gp.affine_select(out=valid[:, 1:2], in_=valid[:, 1:2], compare_op=ALU.is_ge, fill=0.0,
                             base=M1 - 1, pattern=[[0, 1]], channel_multiplier=-1)
            gp.affine_select(out=valid[:, 2:3], in_=valid[:, 2:3], compare_op=ALU.is_ge, fill=0.0,
                             base=TOK - 64 - 1, pattern=[[0, 1]], channel_multiplier=-1)
            gp.affine_select(out=valid_hi[:, 1:2], in_=valid_hi[:, 1:2], compare_op=ALU.is_gt, fill=1.0,
                             base=64, pattern=[[0, 1]], channel_multiplier=-1).then_inc(s["gp_const"], 1)
            gp.wait_ge(s["dve_const"], 1)

            def step(it, par):
                a, b, d, e = it + 2, it + 1, it - 1, it - 2
                for k in range(HEADS):
                    i = k // 2
                    if k == 2 and runs(b):
                        wait_apart(gp, s["mean1"], b * RT + RT, s["filled"])
                        gp.tensor_scalar(ve1[:, :], mv1[:, :, 1], EPS, None, ALU.add).then_inc(s["var1_eps"], 1)
                        wait(gp, s["var1_eps"], b + 1)
                        gp.tensor_tensor(rstd1[:, :], ve1[:, :], minus_half[:, :], ALU.pow).then_inc(s["rstd1_ok"], 1)
                    if runs(a) and k % 2 == 0:
                        for h in range(2):
                            wait(gp, s["mix_act"], a * 16 + 4 * i + h + 1)
                            gp.tensor_tensor(sq[i][:, h, :], xl[i][:, h, :], xl[i][:, h, :], ALU.mult)\
                              .then_inc(s["squared"], 1)
                    if runs(a) and k == 1:
                        wait(gp, s["xin_loaded"], a * 16 + 16)
                        wait(gp, s["z0_act"], a * 2)
                        for h in range(2):
                            gp.tensor_tensor(x_sq[:, h, :], xin[:, h, :], xin[:, h, :], ALU.mult)\
                              .then_inc(s["x_squared"], 1)
                    if k == 5 and runs(d):
                        wait_apart(gp, s["mean2"], d * RT + RT, s["filled"])
                        gp.tensor_scalar(ve2[:, :], mv2[:, :, 1], EPS, None, ALU.add).then_inc(s["var2_eps"], 1)
                        wait(gp, s["var2_eps"], d + 1)
                        gp.tensor_tensor(rstd2[:, :], ve2[:, :], minus_half[:, :], ALU.pow).then_inc(s["rstd2_ok"], 1)
                    if runs(a) and k in (3, 4, 5, 7):
                        n = (3, 4, 5, 7).index(k)
                        for h in range(2):
                            if k == 4:
                                wait(gp, s["z0_act"], a * 2 + h + 1)
                            else:
                                wait(gp, s["mix_act"], a * 16 + 4 * i + h + 3)
                            if n == 0:
                                wait(gp, s["pooled_ok"], a * 2 + h - 1)
                            else:
                                wait(gp, s["z_added"], a * 8 + 2 * (n - 1) + h + 1)
                            left = z[1] if n == 0 else z_sum
                            right = z[0] if k == 4 else z[i + 1]
                            gp.tensor_tensor(z_sum[:, h, :], left[:, h, :], right[:, h, :], ALU.add)\
                              .then_inc(s["z_added"], 1)
                    if k == 5 and runs(e):
                        wait_apart(gp, s["scattered"], e * RT * 16, s["filled"])
                        wait_apart(gp, s["ids_stepped"], e, s["filled"])
                        gp.tensor_copy(ids[:, :], ids_f[:, :]).then_inc(s["ids_ok"], 1)
                        wait_apart(gp, s["ids_ok"], e + 1, s["filled"])
                        gp.tensor_scalar(ids_f[:, :], ids_f[:, :], float(COLS), None, ALU.add).then_inc(s["ids_stepped"], 1)
                        wait_apart(gp, s["placei_ok"], e + 1, s["filled"])
                        if isinstance(e, int) and e == 0:
                            gp.wait_ge(s["lists_cleared"], 16)
                        for t in range(RT):
                            gp.indirect_dma_start(lists, bass.IndirectOffsetOnAxis(ap=place_i[:, t:t + 1], axis=0),
                                                  ids[:, t:t + 1], None, bounds_check=E * CAP - 1,
                                                  oob_is_err=False).then_inc(s["scattered"], 16)

            iterations(gp, step)

            gp.wait_ge(s["rows_stored"], 16 * PAIRS)

            def gather(t, n, turn):
                if not has(t):
                    return
                wait_apart(gp, ids_in[n % LISTED], (turn + 1 + n // LISTED) * 16, s["filled"])
                wait_apart(gp, s["res_ok"], t - BANKED + 1, s["filled"])
                gp.indirect_dma_start(got[n % BANKED][:, :], None, row_store,
                                      bass.IndirectOffsetOnAxis(ap=tile_ids[n % LISTED][:, :], axis=0),
                                      bounds_check=ROWS - 1, oob_is_err=False).then_inc(got_in[n % BANKED], 16)

            def scatter(t, n, turn):
                gather(t + BANKED, n + BANKED, turn)
                wait_apart(gp, s["res_ok"], t + 1, s["filled"])
                gp.indirect_dma_start(out, bass.IndirectOffsetOnAxis(ap=tile_ids[n][:, :], axis=0),
                                      res[n % 2][:, :], None, bounds_check=ROWS - 1,
                                      oob_is_err=False).then_inc(stored[n % 2], 16)

            for t in range(BANKED):
                gather(t, t, 0)
            tiles(gp, scatter)

        @block.scalar
        def _(act):
            act.dma_start(core_sb[:, :], core).then_inc(s["core_loaded"], 16)
            act.dma_start(w_out_sb[:, :, :], w_out).then_inc(s["core_loaded"], 16)
            act.dma_start(b_in_sb[:, :], b_in).then_inc(s["biases"], 16)
            act.dma_start(b_out_sb[:, :], b_out).then_inc(s["biases"], 16)
            act.wait_ge(s["core_loaded"], 32)
            act.activation(core_abs[:, :], core_sb[:, :], ACT.Abs).then_inc(s["core_ready"], 1)
            act.wait_ge(s["core_ready"], 1)
            act.wait_ge(s["biases"], 32)

            def mixer_tanh(a, u):
                i, outer, h = u // 4, (u // 2) % 2, u % 2
                wait(act, s["mix_mm"], a * 16 + u + 1)
                if u == 2:
                    wait(act, s["z_added"], a * 8)
                dst = z[i + 1] if outer else xl[i]
                bias = b_out_sb if outer else b_in_sb
                act.activation(dst[:, h, :], mix_bank(a, u)[:, 0:FRAMES], ACT.Tanh, bias=bias[:, i:i + 1])\
                   .then_inc(s["mix_act"], 1)

            def step(it, par):
                a, b, c, d = it + 2, it + 1, it, it - 1
                for k in range(HEADS):
                    if runs(a):
                        mixer_tanh(a, 2 * k)
                    if runs(c):
                        if k % 2 == 0:
                            wait(act, s["tail_tr"], c * 4 + k // 2 - 1)
                        p, scores = prob[k // 2 % 2], scores_in(c, k)
                        for t in range(RT):
                            if t != 1:
                                wait(act, s["max_ok"], (c * 8 + k) * 2 + t // 2 + 1)
                            bias = neg_max[:, k % 2, t:t + 1]
                            if k % 2 == 0:
                                e = act.activation(p[:, t, 0:TOK], scores[:, t, :], ACT.Exp, bias=bias)
                            else:
                                act.activation(p[:, t, 256:384], scores[:, t, 0:128], ACT.Exp, bias=bias)
                                e = act.activation(p[:, t, 192:192 + M1], scores[:, t, 128:TOK], ACT.Exp, bias=bias)
                            if t != 0:
                                e.then_inc(s["exp_ok"], 1)
                    if runs(a):
                        mixer_tanh(a, 2 * k + 1)
                        if k == 2:
                            for h in range(2):
                                wait(act, s["x_squared"], a * 2 + h + 1)
                                act.activation(z[0][:, h, :], x_sq[:, h, :], ACT.Tanh, scale=core_abs[:, 0:1])\
                                   .then_inc(s["z0_act"], 1)
                    q, two = (d, HEADS // 2 - 1) if k == 0 else (c, k // 2 - 1)
                    if runs(q) and k % 2 == 0:
                        wait(act, s["tail_tr"], q * 4 + two + 1)
                        act.activation(pT1[:, two, :], pT1_ps[:, 0:COLS], ACT.Copy).then_inc(s["pT1_ok"], 1)
                    if k == 4 and runs(b):
                        wait(act, s["h_out"], b + 1)
                        wait(act, s["h2_ok"], (b - 1) * 2)
                        act.activation(h_res[1 - par][:, :, :], h_raw[:, :, :], ACT.Copy).then_inc(s["h_kept"], 1)

            iterations(act, step)

            def xgT_copy(t, n):
                if has(t):
                    wait(act, s["x_tr"], t + 1)
                    wait(act, s["sh_mm"], t - 1)
                    act.activation(xgT[n % 2][:, :], b_ps[:, 0:128], ACT.Copy).then_inc(s["xgT_ok"], 1)

            def activate(t, n):
                if has(t):
                    wait(act, s["up_mm"], t * 2 + 1)
                    wait(act, s["gate_ok"], t)
                    act.activation(half_tanh[:, :], up_ps[n % 2][:, :], ACT.Tanh, scale=0.5).then_inc(s["tanh_ok"], 1)

            def activate_shared(t, n):
                if has(t):
                    wait(act, s["sh_mm"], t + 1)
                    wait(act, s["down_mm"], t - 1)
                    act.activation(shared[n % 2][:, :], sh_ps[:, :], ACT.Gelu).then_inc(s["gelu_ok"], 1)

            def step2(t, n, turn):
                activate(t + 1, n + 1)
                wait(act, s["hid_tr"], t + 1)
                wait(act, s["down_mm"], t)
                act.activation(hidT[:, :], hidT_ps[:, :], ACT.Copy).then_inc(s["hidT_ok"], 1)
                activate_shared(t + 1, n + 1)
                xgT_copy(t + 2, n)

            xgT_copy(0, 0)
            activate(0, 0)
            activate_shared(0, 0)
            xgT_copy(1, 1)
            tiles(act, step2)

        @block.vector
        def _(dve):
            dve.memset(ones[:, :], 1.0)
            dve.memset(minus_half[:, :], -0.5)
            dve.memset(zero8[:, :], 0.0)
            dve.memset(pooled[:, :], 0.0)
            for p in range(2):
                dve.memset(xv[p][:, :, :, 0:HD], 0.0)
                dve.memset(xv[p][:, :, :, HD:HD + 1], 1.0)
                dve.memset(xv[p][:, :, :, HD + 1:VW], 0.0)
                dve.memset(prob[p][:, :, TOK:192], 0.0)
                dve.memset(prob[p][:, :, 192 + M1:256], 0.0)
            dve.memset(rden[:, :], 0.0).then_inc(s["dve_const"], 1)
            dve.wait_ge(s["core_ready"], 1)
            dve.wait_ge(s["core_loaded"], 32)
            for i in range(LAYERS):
                w = dve.tensor_scalar(w_out_c[:, i, :], w_out_sb[:, i, :], core_abs[:, i + 1:i + 2], None, ALU.mult)
            w.then_inc(s["core_ready"], 1)
            dve.wait_ge(s["gp_const"], 8)
            dve.tensor_tensor(valid[:, :], valid[:, :], valid_hi[:, :], ALU.add).then_inc(s["dve_const"], 1)
            dve.wait_ge(s["dve_const"], 2)
            dve.tensor_scalar(pad_far[:, :], valid[:, :], -float(NO_ROW), float(NO_ROW), ALU.mult, ALU.add)\
               .then_inc(s["dve_const"], 1)
            dve.wait_ge(s["dve_const"], 3)

            def layernorm(src, st, mv, stat, mean, n):
                for t in range(RT):
                    dve.bn_stats(st[:, t, :], src[t]).then_inc(s[stat], 1)
                for t in range(RT):
                    wait_apart(dve, s[stat], n * RT + t + 1, s["gp_const"])
                    dve.bn_aggr(mv[:, t, :], st[:, t, :]).then_inc(s[mean], 1)

            def merge(pair, g, p):
                tr = d_ps[:, 0:COLS].rearrange("p (n v) -> p n v", v=VW)
                wait(dve, s["oT_tr"], pair * 2 + g + 1)
                dve.reciprocal(rden[:, :], tr[:, :, HD]).then_inc(s["rden_ok"], 1)
                wait(dve, s["rden_ok"], pair * 2 + g + 1)
                dve.tensor_tensor(attn[:, :, :], tr[:, :, 0:HD],
                                  rden[:, :].rearrange("p (n o) -> p n o", o=1).to_broadcast([128, RT * 4, HD]),
                                  ALU.mult).then_inc(s["attn_ok"], 1)
                wait(dve, s["attn_ok"], pair * 2 + g + 1)
                wait(dve, s["h_kept"], pair + 1)
                if g == 0:
                    wait(dve, s["rows_stored"], pair * 16)
                dve.tensor_tensor(rows[:, :, D + 64 * g:D + 64 * g + 64],
                                  h_res[p][:, :, 64 * g:64 * g + 64],
                                  attn[:, :, :].rearrange("p (t h) v -> p t (h v)", t=RT),
                                  ALU.add).then_inc(s["h2_ok"], 1)

            def pool(b, h):
                wait(dve, s["z_added"], b * 8 + 6 + h + 1)
                if h == 0:
                    wait(dve, s["hT_tr"], b)
                pairs = z_sum[:, h, :].rearrange("p (n two) -> p n two", two=2)
                dve.tensor_tensor(pooled[:, h * HALF:h * HALF + TOK], pairs[:, :, 0], pairs[:, :, 1],
                                  ALU.add).then_inc(s["pooled_ok"], 1)

            def qx_copy(b, j, p):
                wait(dve, s["qx_mm"], b * 8 + j + 1)
                dve.tensor_copy(qx[p][:, j, :], b_ps[:, 0:COLS]).then_inc(s["qx_ok"], 1)

            def step(it, par):
                b, c, d, e = it + 1, it, it - 1, it - 2
                for k in range(HEADS):
                    if k == 2 and runs(e):
                        wait(dve, s["rank_mm"], e + 1)
                        rank = d_ps[:, 0:RT * E].rearrange("p (t e) -> p t e", t=RT)
                        wait(dve, s["next_ok"], e)
                        dve.tensor_tensor(place[:, :, :], rank,
                                          next_place[:, :].rearrange("p (o e) -> p o e", o=1).to_broadcast([128, RT, E]),
                                          ALU.add).then_inc(s["place_ok"], 1)
                        wait(dve, s["place_ok"], e + 1)
                        dve.tensor_tensor(next_place[:, :], next_place[:, :], d_ps[:, RT * E:RT * E + E],
                                          ALU.add).then_inc(s["next_ok"], 1)
                    if k == 6 and runs(d):
                        wait(dve, s["xn2_tr"], d + 1)
                        dve.tensor_copy(xn2T[:, :], d_ps[:, 0:COLS]).then_inc(s["xn2T_ok"], 1)
                    if k == 3 and runs(b):
                        wait(dve, s["xn_tr"], b + 1)
                        dve.tensor_copy(xnT[1 - par][:, :], b_ps[:, 0:COLS]).then_inc(s["xnT_ok"], 1)
                    if k == 7 and runs(d):
                        wait(dve, s["gate_mm"], d + 1)
                        dve.tensor_copy(logits[:, :, :], d_ps[:, 0:RT * E].rearrange("p (t e) -> p t e", t=RT))\
                           .then_inc(s["logits_ok"], 1)
                    if k == 0 and runs(b):
                        pool(b, 0)
                    if k == 2 and runs(b):
                        wait(dve, s["rstd1_ok"], b + 1)
                        for t in range(RT):
                            dve.tensor_scalar(xn[:, t, :], h_raw[:, t, :], mv1[:, t, 0:1], rstd1[:, t:t + 1],
                                              ALU.subtract, ALU.mult).then_inc(s["xn_ok"], 1)
                    if k == 1 and runs(b):
                        wait(dve, s["hT_tr"], b + 1)
                        wait(dve, s["h_kept"], b)
                        dve.tensor_scalar(h_raw[:, :, :], b_ps[:, 0:COLS].rearrange("p (t n) -> p t n", t=RT),
                                          1.0 / (2 * (LAYERS + 1)), None, ALU.mult).then_inc(s["h_out"], 1)
                    if runs(c):
                        for half, (lo, hi) in enumerate(((0, 2), (2, RT))):
                            wait(dve, s["score_mm"], (c * 8 + k) * 2 + half + 1)
                            dve.tensor_reduce(neg_max[:, k % 2, lo:hi], scores_in(c, k)[:, lo:hi, :], AX.X, ALU.max,
                                              negate=True).then_inc(s["max_ok"], 1)
                    if k == 3 and runs(d):
                        wait(dve, s["pv_mm"], d * 2 + 2)
                        dve.tensor_copy(oT[:, 1, :], pv_ps[:, 0:COLS]).then_inc(s["oT_ok"], 1)
                    if k >= 4 and runs(b):
                        qx_copy(b, 2 * k - 7, 1 - par)
                    if k == 0 and runs(b):
                        pool(b, 1)
                    if k == 1 and runs(b):
                        wait(dve, s["h_out"], b + 1)
                        layernorm([h_raw[:, t, :] for t in range(RT)], st1, mv1, "stat1", "mean1", b)
                    q, hd = (d, HEADS - 1) if k == 0 else (c, k - 1)
                    if runs(q):
                        wait(dve, s["pT_tr"], q * 8 + hd + 1)
                        dve.tensor_copy(pT0[:, hd, :], pT0_ps[:, 0:COLS]).then_inc(s["pT0_ok"], 1)
                    if 3 <= k < 7 and runs(b):
                        qx_copy(b, 2 * k - 6, 1 - par)
                    if k == 5 and runs(d):
                        wait(dve, s["rstd2_ok"], d + 1)
                        for t in range(RT):
                            dve.tensor_scalar(rows[:, t, 0:D], rows[:, t, D:2 * D], mv2[:, t, 0:1],
                                              rstd2[:, t:t + 1], ALU.subtract, ALU.mult).then_inc(s["xn2_ok"], 1)
                    if k == 0 and runs(d):
                        merge(d, 0, 1 - par)
                    if k == 2 and runs(e):
                        dve.tensor_tensor(place_of[:, :, :], place[:, :, :], chosen[:, :, :], ALU.mult)\
                           .then_inc(s["placeof_ok"], 1)
                        wait(dve, s["placeof_ok"], e + 1)
                        dve.tensor_reduce(place_f[:, :], place_of[:, :, :], AX.X, ALU.add).then_inc(s["placef_ok"], 1)
                        wait(dve, s["placef_ok"], e + 1)
                        wait(dve, s["scattered"], e * RT * 16)
                        dve.tensor_tensor(place_i[:, :], place_f[:, :], pad_far[:, :], ALU.add)\
                           .then_inc(s["placei_ok"], 1)
                    if k == 3 and runs(d):
                        merge(d, 1, 1 - par)
                    if k == 4 and runs(d):
                        wait(dve, s["h2_ok"], d * 2 + 2)
                        layernorm([rows[:, t, D:2 * D] for t in range(RT)], st2, mv2, "stat2", "mean2", d)
                    if k == 6 and runs(c):
                        wait(dve, s["pv_mm"], c * 2 + 1)
                        dve.tensor_copy(oT[:, 0, :], pv_ps[:, 0:COLS]).then_inc(s["oT_ok"], 1)
                    if k == 7 and runs(d):
                        wait_apart(dve, s["logits_ok"], d + 1, s["gp_const"])
                        for t in range(RT):
                            dve.max(top[:, t, :], logits[:, t, :]).then_inc(s["top_ok"], 1)
                        for t in range(RT):
                            wait_apart(dve, s["top_ok"], d * RT + t + 1, s["gp_const"])
                            dve.max_index(top_i[:, t, :], top[:, t, :], logits[:, t, :]).then_inc(s["topi_ok"], 1)
                        wait(dve, s["topi_ok"], d * RT + RT)
                        dve.tensor_copy(top_f[:, :], top_i[:, :, 0]).then_inc(s["topf_ok"], 1)
                        wait(dve, s["topf_ok"], d + 1)
                        dve.tensor_tensor(is_top[:, :, :],
                                          expert_no[:, :].rearrange("p (o e) -> p o e", o=1).to_broadcast([128, RT, E]),
                                          top_f[:, :].rearrange("p (t o) -> p t o", o=1).to_broadcast([128, RT, E]),
                                          ALU.is_equal).then_inc(s["istop_ok"], 1)
                        wait(dve, s["istop_ok"], d + 1)
                        dve.tensor_tensor(chosen[:, :, :], is_top[:, :, :],
                                          valid[:, :].rearrange("p (t o) -> p t o", o=1).to_broadcast([128, RT, E]),
                                          ALU.mult).then_inc(s["chosen_ok"], 1)
                    if k == 7 and runs(b):
                        wait(dve, s["xv_mm"], b + 1)
                        src = b_ps[:, :].rearrange("p (c h v) -> p c h v", c=4, h=HEADS)
                        dve.tensor_copy(xv[1 - par][:, :, :, 0:HD], src).then_inc(s["xv_ok"], 1)

            iterations(dve, step)

            n = 0

            def done(ins):
                nonlocal n
                n += 1
                ins.then_inc(s["table_step"], 1)
                dve.wait_ge(s["table_step"], n)

            dve.wait_ge(s["next_ok"], PAIRS)
            done(dve.tensor_tensor(count[:, :], next_place[0:1, :], list_start[:, :], ALU.subtract))
            done(dve.tensor_scalar(count_i[:, :], count[:, :], 127.0, None, ALU.add))
            done(dve.tensor_scalar(ntile_i[:, :], count_i[:, :], 7, None, ALU.arith_shift_right))
            done(dve.tensor_copy(ntile[:, :], ntile_i[:, :]))
            done(dve.tensor_tensor_scan(ends[:, :], ntile[:, :], zero8[:, :], 0.0, ALU.add, ALU.add))
            for lo, hi in ((0, LISTED), (LISTED, TILES)):
                def over_tiles(ap):
                    return ap.rearrange("p (o e) -> p o e", o=1).to_broadcast([1, hi - lo, E])

                part = slice(lo, hi)
                done(dve.tensor_tensor(past[:, part, :],
                                       tile_no[:, part].rearrange("p (t o) -> p t o", o=1).to_broadcast([1, hi - lo, E]),
                                       over_tiles(ends[:, :]), ALU.is_ge))
                done(dve.tensor_reduce(t_exp[:, part], past[:, part, :], AX.X, ALU.add))
                done(dve.tensor_tensor(past_n[:, part, :], past[:, part, :], over_tiles(ntile[:, :]), ALU.mult))
                done(dve.tensor_reduce(t_skip[:, part], past_n[:, part, :], AX.X, ALU.add))
                done(dve.tensor_tensor(t_row[:, part], tile_no[:, part], t_skip[:, part], ALU.subtract))
                done(dve.tensor_scalar(t_row2[:, part], t_exp[:, part], float(CAP_TILES), None, ALU.mult))
                dve.tensor_tensor(tab_row[:, part], t_row2[:, part], t_row[:, part], ALU.add)\
                   .then_inc(s["table_ok"], 1)
                dve.tensor_scalar(tab_w[:, part], t_exp[:, part], float(E - 1), float(INNER), ALU.min, ALU.mult)\
                   .then_inc(s["table_ok"], 1)

            def hidden(t, n):
                if not has(t):
                    return
                wait(dve, s["hid_ok"], t)
                wait(dve, s["tanh_ok"], t + 1)
                dve.scalar_tensor_tensor(gate_u[:, :], half_tanh[:, :], 1.0, up_ps[n % 2][:, :], ALU.add, ALU.mult)\
                   .then_inc(s["gate_ok"], 1)
                wait(dve, s["gate_ok"], t + 1)
                wait(dve, s["up_mm"], t * 2 + 2)
                wait(dve, s["hid_tr"], t - 1)
                dve.scalar_tensor_tensor(hid[n % 2][:, :], gate_u[:, :], 0.5, up_ps[2 + n % 2][:, :], ALU.mult, ALU.mult)\
                   .then_inc(s["hid_ok"], 1)

            def step2(t, n, turn):
                hidden(t + 1, n + 1)
                wait(dve, stored[n % 2], (turn * (LISTED // 2) + n // 2) * 16)
                wait(dve, s["down_mm"], t + 1)
                dve.tensor_tensor(res[n % 2][:, :], got[n % BANKED][:, D:2 * D], y_ps[:, 0:D], ALU.add)\
                   .then_inc(s["res_ok"], 1)

            hidden(0, 0)
            tiles(dve, step2)

        @block.tensor
        def _(pe):
            pe.wait_ge(s["mixer_weights"], 16)

            def mixer(a, u):
                i, outer, h = u // 4, (u // 2) % 2, u % 2
                wait(pe, s["mix_act"], mix_free(a, u))
                if outer:
                    if isinstance(a, int) and a == 0 and u == 2:
                        pe.wait_ge(s["core_ready"], 2)
                    wait(pe, s["squared"], a * 8 + 2 * i + h + 1)
                    w, rhs = w_out_c, sq[i]
                else:
                    if i == 0:
                        wait(pe, s["xin_loaded"], a * 16 + 16)
                    w, rhs = w_in_sb, (xin if i == 0 else xl[i - 1])
                pe.matmul(mix_bank(a, u)[:, 0:FRAMES], w[:, i, :], rhs[:, h, :], start=True, stop=True)\
                  .then_inc(s["mix_mm"], 1)

            def three_transposes(dst, src, done):
                for t in range(RT):
                    tr = pe.transpose(dst(t), src(t), ident[:, :])
                tr.then_inc(done, 1)

            def b_piece(b, k, p, late):
                if k == 0 and late:
                    wait(pe, s["pooled_ok"], b * 2 + 2)
                    wait(pe, s["xv_ok"], b)
                    if isinstance(b, int) and b == 0:
                        pe.wait_ge(s["gp_const"], 8)
                    three_transposes(lambda t: b_ps[:, t * 128:t * 128 + 128],
                                     lambda t: pooled[:, t * 128:t * 128 + 128], s["hT_tr"])
                if k == 2 and late:
                    wait(pe, s["xn_ok"], b * RT + RT)
                    three_transposes(lambda t: b_ps[:, t * 128:t * 128 + 128],
                                     lambda t: xn[:, t, :], s["xn_tr"])
                j = 2 * k - 7 + late
                if 0 <= j < HEADS:
                    if j == 0:
                        wait(pe, s["xnT_ok"], b + 1)
                        if isinstance(b, int) and b == 0:
                            pe.wait_ge(s["attn_weights"], 48)
                    else:
                        wait(pe, s["qx_ok"], b * 8 + j)
                    pe.matmul(b_ps[:, 0:COLS], q_sb[:, j, :], xnT[p][:, :], start=True, stop=True)\
                      .then_inc(s["qx_mm"], 1)

            def values(c, p):
                wait(pe, s["qx_ok"], c * 8 + 8)
                for c4, m0, at, m in ((0, 0, 0, 128), (2, HALF, 0, 128), (1, 128, 0, 64), (1, 128, 64, 64),
                                      (3, HALF + 128, 0, 64), (3, HALF + 128, 64, 64)):
                    v = pe.matmul(b_ps[at:at + m, c4 * 128:c4 * 128 + 128], xnT[p][:, m0:m0 + m], v_sb[:, :],
                                  start=True, stop=True)
                v.then_inc(s["xv_mm"], 1)

            def scores_of(c, h, p):
                if h == 0:
                    wait(pe, s["qx_ok"], c * 8 + 8)
                wait(pe, s["exp_ok"], scores_free(c, h) * 2 - 1)
                if isinstance(c, int) and c == PAIRS - 1 and h == 1:
                    pe.wait_ge(s["xv_ok"], PAIRS)
                scores = scores_in(c, h)
                qh, keys = qx[p][:, h, :], (xnT[p][:, 0:TOK], xnT[p][:, HALF:HALF + TOK])
                pe.matmul(scores[:, 0, :], qh[:, 0:128], keys[0], start=True, stop=True)
                pe.matmul(scores[0:64, 1, :], qh[:, 128:192], keys[0], start=True, stop=True)
                pe.matmul(scores[64:128, 1, :], qh[:, 192:256], keys[1], start=True, stop=True)\
                  .then_inc(s["score_mm"], 1)
                wait(pe, s["exp_ok"], scores_free(c, h) * 2)
                pe.matmul(scores[:, 2, :], qh[:, 256:384], keys[1], start=True, stop=True).then_inc(s["score_mm"], 1)

            def probs_T(q, h):
                wait(pe, s["exp_ok"], (q * 8 + h) * 2 + 2)
                wait(pe, s["pT0_ok"], q * 8 + h)
                first = 256 * (h % 2)
                three_transposes(lambda t: pT0_ps[:, t * 128:t * 128 + 128],
                                 lambda t: prob[h // 2 % 2][:, t, first:first + 128], s["pT_tr"])
                if h % 2:
                    wait(pe, s["pT1_ok"], q * 4 + h // 2)
                    three_transposes(lambda t: pT1_ps[:, t * 128:t * 128 + 128],
                                     lambda t: prob[h // 2 % 2][:, t, 128:256], s["tail_tr"])

            def weighted(q, g, p):
                wait(pe, s["xv_ok"], q + 1)
                wait(pe, s["pT0_ok"], q * 8 + 4 * g + 4)
                wait(pe, s["pT1_ok"], q * 4 + 2 * g + 2)
                wait(pe, s["oT_ok"], q * 2 + g)
                for half in range(2):
                    cols = slice(half * HALF, half * HALF + HALF)
                    for j in range(4):
                        h = 4 * g + j
                        pe.matmul(pv_ps[32 * j:32 * j + VW, cols], xv[p][:, 2 * half, h, :],
                                  pT0[:, h, cols], start=True, stop=False)
                    for j in range(4):
                        h = 4 * g + j
                        keys = slice(64 * (h % 2), 64 * (h % 2) + M1)
                        v = pe.matmul(pv_ps[32 * j:32 * j + VW, cols], xv[p][keys, 2 * half + 1, h, :],
                                      pT1[keys, h // 2, cols], start=False, stop=True)
                v.then_inc(s["pv_mm"], 1)

            def heads_T(q, g):
                wait(pe, s["oT_ok"], q * 2 + g + 1)
                three_transposes(lambda t: d_ps[:, t * 128:t * 128 + 128],
                                 lambda t: oT[:, g, t * 128:t * 128 + 128], s["oT_tr"])

            def rank(e):
                wait(pe, s["chosen_ok"], e + 1)
                wait(pe, s["attn_ok"], e * 2 + 3 if not isinstance(e, int) or e + 1 < PAIRS else e * 2 + 2)
                for t in range(RT):
                    for t2 in range(t):
                        pe.matmul(d_ps[:, t * E:t * E + E], ones[:, :], chosen[:, t2, :],
                                  start=(t2 == 0), stop=False)
                    pe.matmul(d_ps[:, t * E:t * E + E], before[:, :], chosen[:, t, :],
                              start=(t == 0), stop=True)
                for t in range(RT):
                    m = pe.matmul(d_ps[:, RT * E:RT * E + E], ones[:, :], chosen[:, t, :],
                                  start=(t == 0), stop=(t == RT - 1))
                m.then_inc(s["rank_mm"], 1)

            def late_unit(it, k, p):
                a, b = it + 2, it + 1
                if runs(b) and k != 1:
                    b_piece(b, k, p, 1)
                if runs(a):
                    mixer(a, 2 * k + 1)
                if runs(b) and k == 1:
                    b_piece(b, k, p, 1)

            def step(it, par):
                a, b, c, d, e = it + 2, it + 1, it, it - 1, it - 2
                for k in range(HEADS):
                    if runs(c):
                        scores_of(c, k, par)
                    if k == 7 and runs(a):
                        mixer(a, 2 * k)
                    if runs(b):
                        b_piece(b, k, 1 - par, 0)
                    if k < 7 and runs(a):
                        mixer(a, 2 * k)
                    q, h = (d, HEADS - 1) if k == 0 else (c, k - 1)
                    if runs(q):
                        probs_T(q, h)
                    if k == 7 and runs(c):
                        if runs(d):
                            wait(pe, s["logits_ok"], d + 1)
                        heads_T(c, 0)
                    if k not in (1, 2):
                        late_unit(it, k, 1 - par)
                    if k == 1 and runs(e):
                        rank(e)
                    if k == 1 and runs(d):
                        weighted(d, 1, 1 - par)
                    if k == 3 and runs(d):
                        wait(pe, s["next_ok"], d)
                        heads_T(d, 1)
                    if k in (1, 2):
                        late_unit(it, k, 1 - par)
                    if k == 5 and runs(c):
                        weighted(c, 0, par)
                    if k == 5 and runs(d):
                        wait(pe, s["xn2_ok"], d * RT + RT)
                        three_transposes(lambda t: d_ps[:, t * 128:t * 128 + 128],
                                         lambda t: rows[:, t, 0:D], s["xn2_tr"])
                    if k == 6 and runs(d):
                        wait(pe, s["xn2T_ok"], d + 1)
                        for t in range(RT):
                            g = pe.matmul(d_ps[:, t * E:t * E + E], xn2T[:, t * 128:t * 128 + 128],
                                          gate_sb[:, :], start=True, stop=True)
                        g.then_inc(s["gate_mm"], 1)
                    if k == 7 and runs(b):
                        values(b, 1 - par)

            iterations(pe, step)

            pe.wait_ge(s["expert_weights"], 48)
            pe.wait_ge(s["shared_weights"], 32)
            pe.wait_ge(s["table_ok"], 4)

            def expert(t):
                return pe.value_load(tab_w[0:1, bass.ds(t, 1)], min_val=0, max_val=(E - 1) * INNER)

            def rows_T(t, n, turn):
                if has(t):
                    pe.wait_ge(got_in[n % BANKED], (turn * (LISTED // BANKED) + n // BANKED + 1) * 16)
                    wait(pe, s["xgT_ok"], t)
                    pe.transpose(b_ps[:, 0:128], got[n % BANKED][:, 0:D], ident[:, :]).then_inc(s["x_tr"], 1)

            def up(t, n):
                if not has(t):
                    return
                w = expert(t)
                wait(pe, s["xgT_ok"], t + 1)
                wait(pe, s["hid_ok"], t - 1)
                for i, w_sb in enumerate((w1_sb, w3_sb)):
                    pe.matmul(up_ps[2 * i + n % 2][:, :], xgT[n % 2][:, :], w_sb[:, bass.ds(w, INNER)],
                              start=True, stop=True).then_inc(s["up_mm"], 1)
                return w

            def up_shared(t, n):
                if not has(t):
                    return
                wait(pe, s["gelu_ok"], t)
                for c in range(NC):
                    m = pe.matmul(sh_ps[:, c * 128:c * 128 + 128], sw1_sb[:, c * 128:c * 128 + 128],
                                  xgT[n % 2][:, :], start=True, stop=True)
                m.then_inc(s["sh_mm"], 1)

            def step2(t, n, turn):
                nonlocal w_held
                w, w_held = w_held, up(t + 1, n + 1)
                wait(pe, s["hid_ok"], t + 1)
                wait_apart(pe, s["hidT_ok"], t, s["table_ok"])
                for c in range(NC):
                    tr = pe.transpose(hidT_ps[:, c * 128:c * 128 + 128], hid[n % 2][:, c * 128:c * 128 + 128],
                                      ident[:, :])
                tr.then_inc(s["hid_tr"], 1)
                up_shared(t + 1, n + 1)
                rows_T(t + 2, n + 2, turn)
                if n == 0:
                    w = expert(t)
                wait(pe, s["gelu_ok"], t + 1)
                wait(pe, s["res_ok"], t)
                for c in range(NC):
                    pe.matmul(y_ps[:, 0:D], shared[n % 2][:, c * 128:c * 128 + 128],
                              sw2_sb[:, c * 128:c * 128 + 128], start=(c == 0), stop=False)
                wait(pe, s["hidT_ok"], t + 1)
                for c in range(NC):
                    m = pe.matmul(y_ps[:, 0:D], hidT[:, c * 128:c * 128 + 128],
                                  w2_sb[:, bass.ds(w + c * 128, 128)], start=False, stop=(c == NC - 1))
                m.then_inc(s["down_mm"], 1)

            rows_T(0, 0, 0)
            w_held = None
            up(0, 0)
            up_shared(0, 0)
            rows_T(1, 1, 0)
            tiles(pe, step2)


def kernel(**inputs):
    import numpy as np
    import concourse.bacc as bacc
    from concourse.bass_utils import run_bass_kernel_spmd

    def lay(name, *order):
        return np.asarray(inputs[name]).transpose(order)

    x = np.asarray(inputs["x"])[:, :FRAMES, :]
    arrays = {
        "xT": x.transpose(2, 0, 1).reshape(D, BATCH * FRAMES),
        "w_in": lay("L0_tok_W_in", 1, 0, 2),
        "b_in": lay("L0_tok_b_in", 1, 0),
        "w_out": lay("L0_tok_W_out", 1, 0, 2),
        "b_out": lay("L0_tok_b_out", 1, 0),
        "core": lay("L0_tok_core_diag", 1, 0),
        "q_w": lay("L0_attn_Q", 1, 0, 2),
        "v_w": lay("L0_attn_V", 1, 0, 2).reshape(D, HEADS * HD),
        "gate_w": lay("L0_ffn_gate_w", 1, 0),
        "w1": lay("L0_ffn_w1", 2, 0, 1).reshape(D, E * INNER),
        "w3": lay("L0_ffn_w3", 2, 0, 1).reshape(D, E * INNER),
        "w2": np.asarray(inputs["L0_ffn_w2"]).reshape(E, D, NC, 128).transpose(3, 0, 2, 1).reshape(128, E * INNER),
        "sw1": lay("L0_ffn_sw1", 1, 0),
        "sw2": np.asarray(inputs["L0_ffn_sw2"]).reshape(D, NC, 128).transpose(2, 1, 0).reshape(128, INNER),
    }
    nc = bacc.Bacc("TRN2", target_bir_lowering=False, num_devices=1)
    feed, args = {}, []
    for name, a in arrays.items():
        a = np.ascontiguousarray(a)
        feed[f"in_{name}"] = a
        args.append(nc.dram_tensor(f"in_{name}", a.shape, mybir.dt.from_np(a.dtype), kind="ExternalInput").ap())
    args.append(nc.dram_tensor("out_rows", (ROWS, D), F32, kind="ExternalOutput").ap())
    tower(nc, *args)
    r = run_bass_kernel_spmd(nc, [feed], core_ids=[0])
    rows = r.results[0]["out_rows"].reshape(BATCH, HALF, D)
    return rows[:, :TOK, :]
```
